# Optimizing a Trainium2 kernel written in Bass

```python
import numpy as np
import jax
import jax.numpy as jnp

def _softmax(x, axis=-1):
    return jax.nn.softmax(x, axis=axis)

def _gelu(x):
    return jax.nn.gelu(x, approximate=True)

def _silu(x):
    return jax.nn.silu(x)

def _sigmoid(x):
    return jax.nn.sigmoid(x)

def _layernorm(x, axis=-1, eps=1e-05):
    m = jnp.mean(x, axis=axis, keepdims=True)
    v = jnp.var(x, axis=axis, keepdims=True)
    return (x - m) / jnp.sqrt(v + eps)

def _scatter_add(tgt, idx, src, axis=0):
    return tgt.at[idx].add(src)

def _segment_sum(src, seg, n):
    return jax.ops.segment_sum(src, seg, n)
kernel_name = 'mk_adaln_d1_jaxref_r8_b2a806'

def setup_inputs(seed: int=0):
    np.random.seed(seed)
    _w = jnp.asarray

    def _L0_attn_setup():
        import jax, jax.numpy as jnp
        import numpy as np
        H = 32
        G = 8
        D = 128
        HID = 512
        THETA = 10000.0

        def _rope(x, pos):
            half = D // 2
            inv_freq = 1.0 / THETA ** (jnp.arange(0, half, dtype=jnp.float32) / half)
            ang = pos[:, None].astype(jnp.float32) * inv_freq[None, :]
            cos = jnp.cos(ang)[None, None]
            sin = jnp.sin(ang)[None, None]
            x1, x2 = (x[..., :half], x[..., half:])
            return jnp.concatenate([x1 * cos - x2 * sin, x1 * sin + x2 * cos], axis=-1)
        key = jax.random.key(seed)
        ks = jax.random.split(key, 9)
        s = 0.02
        return {'hidden_states': jax.random.normal(ks[0], (1, 256, HID), jnp.float32), 'Wq': jax.random.normal(ks[1], (HID, H * D), jnp.float32) * s, 'bq': jnp.zeros((H * D,), jnp.float32), 'Wk': jax.random.normal(ks[2], (HID, G * D), jnp.float32) * s, 'bk': jnp.zeros((G * D,), jnp.float32), 'Wv': jax.random.normal(ks[3], (HID, G * D), jnp.float32) * s, 'bv': jnp.zeros((G * D,), jnp.float32), 'Wo': jax.random.normal(ks[4], (H * D, HID), jnp.float32) * s, 'bo': jnp.zeros((HID,), jnp.float32)}
    _L0_attn_in = _L0_attn_setup()

    def _L0_ffn_setup():
        import jax, jax.numpy as jnp
        import numpy as np
        B, S, D_IN, D_OUT = (2, 256, 512, 512)
        E, K, R = (8, 2, 16)
        SCALING = 32.0 / 16.0
        key = jax.random.key(seed)
        ks = jax.random.split(key, 6)
        x = jax.random.normal(ks[0], (B, S, D_IN), dtype=jnp.float32)
        gate_w = jax.random.normal(ks[1], (E, D_IN), dtype=jnp.float32) * 0.02
        base_w = jax.random.normal(ks[2], (D_OUT, D_IN), dtype=jnp.float32) * 0.02
        base_b = jax.random.normal(ks[3], (D_OUT,), dtype=jnp.float32) * 0.02
        lora_A = jax.random.normal(ks[4], (E, R, D_IN), dtype=jnp.float32) * 0.02
        lora_B = jax.random.normal(ks[5], (E, D_OUT, R), dtype=jnp.float32) * 0.02
        return {'x': x, 'gate_w': gate_w, 'base_w': base_w, 'base_b': base_b, 'lora_A': lora_A, 'lora_B': lora_B}
    _L0_ffn_in = _L0_ffn_setup()
    _L0_c = _w((lambda *s: np.random.randn(*s).astype(np.float32) * 0.05)(2, 512))
    _L0_wmod = _w((lambda *s: np.random.randn(*s).astype(np.float32) * 0.05)(512, 6 * 512) * 512 ** (-0.5))
    _d = {'L0_attn_hidden_states': _L0_attn_in['hidden_states'], 'L0_attn_Wq': _L0_attn_in['Wq'], 'L0_attn_bq': _L0_attn_in['bq'], 'L0_attn_Wk': _L0_attn_in['Wk'], 'L0_attn_bk': _L0_attn_in['bk'], 'L0_attn_Wv': _L0_attn_in['Wv'], 'L0_attn_bv': _L0_attn_in['bv'], 'L0_attn_Wo': _L0_attn_in['Wo'], 'L0_attn_bo': _L0_attn_in['bo'], 'L0_ffn_gate_w': _L0_ffn_in['gate_w'], 'L0_ffn_base_w': _L0_ffn_in['base_w'], 'L0_ffn_base_b': _L0_ffn_in['base_b'], 'L0_ffn_lora_A': _L0_ffn_in['lora_A'], 'L0_ffn_lora_B': _L0_ffn_in['lora_B'], 'L0_c': _L0_c, 'L0_wmod': _L0_wmod}
    _x0 = _d['L0_attn_hidden_states']
    _d['L0_attn_hidden_states'] = jax.random.normal(jax.random.fold_in(jax.random.key(seed), 1), (2, 512, 512), dtype=_x0.dtype)
    del _x0
    return _d

def reference(L0_attn_hidden_states, L0_attn_Wq, L0_attn_bq, L0_attn_Wk, L0_attn_bk, L0_attn_Wv, L0_attn_bv, L0_attn_Wo, L0_attn_bo, L0_ffn_gate_w, L0_ffn_base_w, L0_ffn_base_b, L0_ffn_lora_A, L0_ffn_lora_B, L0_c, L0_wmod):

    def _L0_attn_ref(hidden_states, Wq, bq, Wk, bk, Wv, bv, Wo, bo):
        import jax, jax.numpy as jnp
        import numpy as np
        H = 32
        G = 8
        D = 128
        HID = 512
        THETA = 10000.0

        def _rope(x, pos):
            half = D // 2
            inv_freq = 1.0 / THETA ** (jnp.arange(0, half, dtype=jnp.float32) / half)
            ang = pos[:, None].astype(jnp.float32) * inv_freq[None, :]
            cos = jnp.cos(ang)[None, None]
            sin = jnp.sin(ang)[None, None]
            x1, x2 = (x[..., :half], x[..., half:])
            return jnp.concatenate([x1 * cos - x2 * sin, x1 * sin + x2 * cos], axis=-1)
        B, S, _ = hidden_states.shape
        R = H // G
        q = hidden_states @ Wq + bq
        k = hidden_states @ Wk + bk
        v = hidden_states @ Wv + bv
        q = q.reshape(B, S, H, D).transpose(0, 2, 1, 3)
        k = k.reshape(B, S, G, D).transpose(0, 2, 1, 3)
        v = v.reshape(B, S, G, D).transpose(0, 2, 1, 3)
        pos = jnp.arange(S)
        q = _rope(q, pos)
        k = _rope(k, pos)
        qg = q.reshape(B, G, R, S, D)
        scores = jnp.einsum('bgrsd,bgtd->bgrst', qg, k) / jnp.sqrt(jnp.float32(D))
        causal = jnp.tril(jnp.ones((S, S), dtype=bool))
        scores = jnp.where(causal[None, None, None], scores, jnp.finfo(scores.dtype).min)
        probs = jax.nn.softmax(scores, axis=-1)
        ctx = jnp.einsum('bgrst,bgtd->bgrsd', probs, v)
        ctx = ctx.reshape(B, H, S, D).transpose(0, 2, 1, 3).reshape(B, S, H * D)
        return ctx @ Wo + bo

    def _L0_ffn_ref(x, gate_w, base_w, base_b, lora_A, lora_B):
        import jax, jax.numpy as jnp
        import numpy as np
        B, S, D_IN, D_OUT = (2, 256, 512, 512)
        E, K, R = (8, 2, 16)
        SCALING = 32.0 / 16.0
        gate_logits = jnp.einsum('bsd,ed->bse', x, gate_w)
        weights, selected = jax.lax.top_k(gate_logits, K)
        weights = jax.nn.softmax(weights.astype(jnp.float32), axis=2).astype(x.dtype)
        result = jnp.einsum('bsd,od->bso', x, base_w) + base_b
        w_full = jnp.sum(jax.nn.one_hot(selected, E, dtype=x.dtype) * weights[..., None], axis=2)
        low = jnp.einsum('bsd,erd->ebsr', x, lora_A)
        lora_out = jnp.einsum('ebsr,eor,bse->bso', low, lora_B, w_full)
        result = result + SCALING * lora_out
        return result
    x = L0_attn_hidden_states
    mod = (_silu(L0_c) @ L0_wmod).reshape(L0_c.shape[0], 6, 1, -1)
    sa, ca, ga, sb, cb, gb = (mod[:, 0], mod[:, 1], mod[:, 2], mod[:, 3], mod[:, 4], mod[:, 5])
    ga = (2 * (ga >= 0) - 1) * jnp.maximum(jnp.abs(ga), 0.25)
    gb = (2 * (gb >= 0) - 1) * jnp.maximum(jnp.abs(gb), 0.25)
    h = _layernorm(x, axis=-1) * (1 + ca) + sa
    x = x + ga * _L0_attn_ref(h, L0_attn_Wq, L0_attn_bq, L0_attn_Wk, L0_attn_bk, L0_attn_Wv, L0_attn_bv, L0_attn_Wo, L0_attn_bo)
    h = _layernorm(x, axis=-1) * (1 + cb) + sb
    x = x + gb * _L0_ffn_ref(h, L0_ffn_gate_w, L0_ffn_base_w, L0_ffn_base_b, L0_ffn_lora_A, L0_ffn_lora_B)
    return x

_drawn_inputs = setup_inputs


def setup_inputs(seed=0):
    import zlib

    import numpy as np

    out = dict(_drawn_inputs(seed))
    spreads = {'L0_attn_bq': (0.0, 0.8),
     'L0_attn_bk': (0.0, 0.8),
     'L0_attn_bv': (0.0, 0.1),
     'L0_attn_bo': (0.0, 0.329)}
    factors = {'L0_attn_Wq': 8.0,
     'L0_attn_Wk': 8.0,
     'L0_attn_Wv': 3.457,
     'L0_ffn_gate_w': 5.123,
     'L0_ffn_base_b': 8.0,
     'L0_ffn_lora_A': 4.364,
     'L0_ffn_lora_B': 4.351}
    for name, (base, spread) in spreads.items():
        noise = np.random.default_rng([zlib.crc32(name.encode()), seed]).standard_normal(out[name].shape)
        drawn = base * np.exp(spread * noise) if base else spread * noise
        out[name] = jnp.asarray(drawn.astype(out[name].dtype))
    for name, factor in factors.items():
        out[name] = (out[name] * factor).astype(out[name].dtype)
    return out
```

```python
from contextlib import ExitStack

import concourse.bass as bass
from concourse import mybir

B, S, HID = 2, 512, 512
H, G, D = 32, 8, 128
R = H // G
P = 128
KT = HID // P
NT = S // P
E, RANK = 8, 16
EPS = 1e-5
SCALE = float(D) ** -0.5
MASKED = -(2.0 ** 127)
SLOTS = B * NT
TRI = [0, 1, 3, 6, 10]
ITEMS = 2 + R
ROPES = 1 + R
K_, V_, Q_ = 0, 1, 2
LORA_PAD = 256
SPLIT_AT = {(0, 0): K_, (0, 1): V_, (0, 2): Q_, (0, 3): Q_ + 1, (1, 0): Q_ + 2, (1, 1): Q_ + 3}

F32 = mybir.dt.float32
F32R = mybir.dt.float32r
U32 = mybir.dt.uint32
ALU = mybir.AluOpType
ACT = mybir.ActivationFunctionType


def adaln_block(nc, x, Wq, Wk, Wv, Wo, bq, bk, bv, bo, gateT, baseT, base_b, loraAT, loraB, c, wmod,
                consts, iota8, out):
    ctx = ExitStack()
    with ctx:
        def sb(name, shape, dt=F32, stack=ctx):
            return stack.enter_context(nc.sbuf_tensor(name, shape, dt))

        def sem(name):
            return ctx.enter_context(nc.semaphore(name))

        const = sb("const", [P, 3 * S + P])
        cos = const[:, 0:S]
        sin = const[:, S:2 * S]
        mask = const[:, 2 * S:3 * S]
        ident = const[:, 3 * S:3 * S + P]
        acc = sb("acc", [P, B * NT, HID])
        cT = sb("cT", [P, B, KT])
        siluT = sb("siluT", [P, KT, B])
        modT = sb("modT", [P, 6, KT, B])
        stats = sb("stats", [P, B * NT, 6])
        mv = sb("mv", [P, B * NT, 2])
        var = sb("var", [P, B * NT])
        rstd = sb("rstd", [P, B * NT])
        half = sb("half", [P, B * NT])
        bq_sb = sb("bq_sb", [P, H])
        bk_sb = sb("bk_sb", [P, G])
        bv_sb = sb("bv_sb", [P, G])
        negmax = sb("negmax", [P, 2, R])
        rowsum = sb("rowsum", [P, 2, R])
        rinv = sb("rinv", [P, 2, R])
        PS = [ctx.enter_context(nc.psum_tensor(f"bank{k}", [P, 512], F32)) for k in range(8)]
        s_bank = [PS[0], PS[1], PS[2], PS[0]]
        pt_bank = [PS[3], PS[4]]
        ctx_bank = PS[5]
        A_, B_ = PS[6], PS[7]

        s_x = [sem(f"s_x{b}") for b in range(B)]
        s_const, s_c, s_bias, s_bo = sem("s_const"), sem("s_c"), sem("s_bias"), sem("s_bo")
        s_wm = [sem(f"s_wm{k}") for k in range(2)]
        s_rawk, s_rawv, s_rawq, s_rawo = sem("s_rawk"), sem("s_rawv"), sem("s_rawq"), sem("s_rawo")
        s_expc, s_silu = sem("s_expc"), sem("s_silu")
        s_modp, s_mod = sem("s_modp"), sem("s_mod")
        s_half, s_var, s_rstd = sem("s_half"), sem("s_var"), sem("s_rstd")
        s_dve = sem("s_dve")
        s_xn, s_xnT, s_ht, s_hhi, s_hlo = sem("s_xn"), sem("s_xnT"), sem("s_ht"), sem("s_hhi"), sem("s_hlo")
        s_whi, s_wlo, s_wohi, s_wolo = sem("s_whi"), sem("s_wlo"), sem("s_wohi"), sem("s_wolo")
        s_proj, s_rope, s_rot, s_qkhi, s_qklo = sem("s_proj"), sem("s_rope"), sem("s_rot"), sem("s_qkhi"), sem("s_qklo")
        s_vt, s_vtr, s_vhi, s_vlo = sem("s_vt"), sem("s_vtr"), sem("s_vhi"), sem("s_vlo")
        s_scores, s_negmax, s_exp, s_rinv, s_prob = sem("s_scores"), sem("s_negmax"), sem("s_exp"), sem("s_rinv"), sem("s_prob")
        s_pt, s_pthi, s_ptlo = sem("s_pt"), sem("s_pthi"), sem("s_ptlo")
        s_ctx, s_ctxhi, s_ctxlo, s_o, s_acc = sem("s_ctx"), sem("s_ctxhi"), sem("s_ctxlo"), sem("s_o"), sem("s_acc")

        with ExitStack() as attn:
            hThi = sb("hThi", [P, KT, B * S], F32R, attn)
            hTlo = sb("hTlo", [P, KT, B * S], F32R, attn)
            wqkv = {hl: sb(f"wqkv{hl}", [P, ITEMS, KT, P], F32R, attn) for hl in ("hi", "lo")}
            wo = {hl: sb(f"wo{hl}", [P, R, HID], F32R, attn) for hl in ("hi", "lo")}
            rawk = sb("rawk", [P, KT, P], F32, attn)
            rawv = sb("rawv", [P, KT, P], F32, attn)
            rawq = sb("rawq", [P, KT, R * P], F32, attn)
            rawo = sb("rawo", [P, R, HID], F32, attn)
            qkhi = sb("qkhi", [P, 2, ROPES, S], F32R, attn)
            qklo = sb("qklo", [P, 2, ROPES, S], F32R, attn)
            vt = sb("vt", [P, S], F32, attn)
            vhi = sb("vhi", [P, 2, NT, P], F32R, attn)
            vlo = sb("vlo", [P, 2, NT, P], F32R, attn)
            prob = [sb("prob0", [P, R, 3 * P], F32, attn), sb("prob1", [P, R, 4 * P], F32, attn)]
            pthi = sb("pthi", [P, NT, R * P], F32R, attn)
            ptlo = sb("ptlo", [P, NT, R * P], F32R, attn)
            ctxhi = sb("ctxhi", [P, R * P], F32R, attn)
            ctxlo = sb("ctxlo", [P, R * P], F32R, attn)
            ropeA = sb("ropeA", [P, 2, S], F32, attn)
            ropeB = sb("ropeB", [P, 2, S], F32, attn)
            xn = [prob[1], acc[:, NT:2 * NT, :]]
            ht = [vt, prob[0][:, :, :].rearrange("p a n -> p (a n)")[:, 0:S]]

            def raw_item(k):
                if k == K_:
                    return rawk[:, :, :]
                if k == V_:
                    return rawv[:, :, :]
                return rawq[:, :, (k - Q_) * P:(k - Q_ + 1) * P]

            def wait_raw(eng, g, k):
                eng.wait_ge(s_rawk if k == K_ else s_rawv if k == V_ else s_rawq, 16 * g + 16)

            def slot(g, b, i):
                return g * SLOTS + (NT * b + i)

            def unit(g, b):
                return g * B + b

            def pts(g, b, i):
                return g * (2 * TRI[NT]) + (b * TRI[NT] + TRI[i])

            def following(g, b, i):
                i += 1
                if i == NT:
                    i, b = 0, b + 1
                if b == B:
                    b, g = 0, g + 1
                return g, b, i

            def ahead(g, b, i, last):
                gn, bn = (g, 1) if b == 0 else (g + 1, 0)
                if i == NT - 1:
                    return ([] if last else [(g + 1, b, K_, A_)]), B_
                if last and b == 1:
                    return [], (A_ if i < 2 else B_)
                return {0: ([(gn, bn, V_, A_), (gn, bn, Q_, B_)], A_),
                        1: ([(gn, bn, Q_ + 1, A_), (gn, bn, Q_ + 2, B_)], A_),
                        2: ([(gn, bn, Q_ + 3, A_)], B_)}[i]

            def rope_no(k):
                return 0 if k == K_ else k - 1

            def parity(b, r):
                return (b * ROPES + r) % 2

            main = attn.enter_context(nc.Block())

            @main.sync
            def _(sp):
                xv = x.rearrange("b (t p) n -> b p t n", p=P)
                sp.dma_start(acc[:, 0:NT, :], xv[0]).then_inc(s_x[0], 16)
                sp.dma_start(cT[:, :, :], c.rearrange("b (p t) -> p b t", t=KT)).then_inc(s_c, 16)
                sp.dma_start(const[:, :], consts).then_inc(s_const, 16)
                wms = wmod.rearrange("(p t) n -> p t n", t=KT)
                sp.dma_start(rawo[:, :, :], wms[:, :, 0:HID]).then_inc(s_wm[0], 16)
                for t in range(KT):
                    half = (ropeA, ropeB)[t // 2]
                    sp.dma_start(half[:, t % 2, :], wms[:, t, HID:2 * HID]).then_inc(s_wm[1], 16)
                sp.dma_start(bq_sb[:, :], bq).then_inc(s_bias, 16)
                sp.dma_start(bk_sb[:, :], bk).then_inc(s_bias, 16)
                sp.dma_start(bv_sb[:, :], bv).then_inc(s_bias, 16)
                sp.dma_start(rawk[:, :, :], Wk[0]).then_inc(s_rawk, 16)
                sp.dma_start(rawv[:, :, :], Wv[0]).then_inc(s_rawv, 16)
                sp.dma_start(rawq[:, :, :], Wq[0]).then_inc(s_rawq, 16)
                sp.dma_start(acc[:, NT:2 * NT, :], xv[1]).then_inc(s_x[1], 16)
                sp.wait_ge(s_modp, 1)
                sp.dma_start(rawo[:, :, :], Wo[0]).then_inc(s_rawo, 16)
                sp.wait_ge(s_xnT, B * KT)
                for t in range(B * NT):
                    sp.dma_start(acc[:, t, :], bo.broadcast_to([P, HID])).then_inc(s_bo, 16)

                def loads(g):
                    sp.wait_ge(s_wlo, g * ITEMS + ITEMS)
                    sp.dma_start(rawk[:, :, :], Wk[bass.ds(g + 1, 1)]).then_inc(s_rawk, 16)
                    sp.dma_start(rawv[:, :, :], Wv[bass.ds(g + 1, 1)]).then_inc(s_rawv, 16)
                    sp.dma_start(rawq[:, :, :], Wq[bass.ds(g + 1, 1)]).then_inc(s_rawq, 16)
                    sp.wait_ge(s_wolo, g * R + R)
                    sp.dma_start(rawo[:, :, :], Wo[bass.ds(g + 1, 1)]).then_inc(s_rawo, 16)

                with sp.Fori(0, G - 1) as g:
                    loads(g)
                sp.wait_ge(s_bo, 16 * B * NT)

            @main.tensor
            def _(pe):
                def three(out, whi, wlo, xhi, xlo, start, stop):
                    nc.tensor.matmul(out, whi, xhi, start=start, stop=False)
                    nc.tensor.matmul(out, whi, xlo, start=False, stop=False)
                    return nc.tensor.matmul(out, wlo, xhi, start=False, stop=stop)

                def project(g, b, k, bank):
                    pe.wait_ge(s_wlo, g * ITEMS + (k + 1))
                    for t in range(KT):
                        last = three(bank[:, :], wqkv["hi"][:, k, t, :], wqkv["lo"][:, k, t, :],
                                     hThi[:, t, b * S:(b + 1) * S], hTlo[:, t, b * S:(b + 1) * S],
                                     t == 0, t == KT - 1)
                    last.then_inc(s_proj, 1)

                def turn_v(g, b):
                    pe.wait_ge(s_vt, unit(g, b) + 1)
                    for t in range(NT):
                        last = nc.tensor.transpose(pt_bank[1][:, t * P:(t + 1) * P], vt[:, t * P:(t + 1) * P], ident)
                    last.then_inc(s_vtr, 1)

                def scores(g, b, i, h, first=False):
                    n = slot(g, b, i)
                    if i == 0:
                        pe.wait_ge(s_qklo, unit(g, b) * ROPES + (h + 2))
                    if not first or h == 3:
                        pe.wait_ge(s_exp, {0: n * R, 1: n * R - 2, 2: n * R - 1, 3: n * R + 1}[h])
                    w = max(2, i + 1) * P
                    q = slice(i * P, (i + 1) * P)
                    three(s_bank[h][:, 0:w], qkhi[:, b, 1 + h, q], qklo[:, b, 1 + h, q],
                          qkhi[:, b, 0, 0:w], qklo[:, b, 0, 0:w], True, True).then_inc(s_scores, 1)

                def turn(g, b, i, j):
                    if j == 0:
                        pe.wait_ge(s_prob, slot(g, b, i) * R + R)
                    if j == 1 and i == 1 and vt_ahead:
                        pe.wait_ge(s_vlo, unit(g, b) + 2)
                    if j >= 2:
                        pe.wait_ge(s_ptlo, pts(g, b, i) + (j - 1))
                    for h in range(R):
                        last = nc.tensor.transpose(pt_bank[j % 2][:, h * P:(h + 1) * P],
                                                   prob[i % 2][:, h, j * P:(j + 1) * P], ident)
                    last.then_inc(s_pt, 1)

                def values(g, b, i):
                    for j in range(i + 1):
                        pe.wait_ge(s_ptlo, pts(g, b, i) + (j + 1))
                        last = three(ctx_bank[:, :], vhi[:, b, j, :], vlo[:, b, j, :],
                                     pthi[:, j, :], ptlo[:, j, :], j == 0, j == i)
                    last.then_inc(s_ctx, 1)

                def output(g, b, i, bank):
                    if (b, i) == (0, 0):
                        pe.wait_ge(s_wolo, g * R + R)
                    pe.wait_ge(s_ctxlo, slot(g, b, i) + 1)
                    for h in range(R):
                        last = three(bank[:, :], ctxhi[:, h * P:(h + 1) * P], ctxlo[:, h * P:(h + 1) * P],
                                     wo["hi"][:, h, :], wo["lo"][:, h, :], h == 0, h == R - 1)
                    last.then_inc(s_o, 1)

                def bank_free(g, b, i, what):
                    n, ropes = slot(g, b, i), (unit(g, b) + 1) * ROPES
                    if what == "out":
                        if not items or i == 3:
                            pe.wait_ge(s_acc, n + 1)
                        elif i == 0:
                            pe.wait_ge(s_vt, unit(g, b) + 2)
                        else:
                            pe.wait_ge(s_rope, ropes + 2 * i)
                            if i == 1:
                                pe.wait_ge(s_rope, ropes + 3)
                    elif (i, what) == (0, V_):
                        pe.wait_ge(s_rope, ropes + 1)
                    elif (i, what) == (1, Q_ + 2):
                        pe.wait_ge(s_rope, ropes + 2)
                    elif (i, what) == (3, K_):
                        pe.wait_ge(s_rope, ropes + 5)
                    else:
                        pe.wait_ge(s_acc, n + 1)

                pe.wait_ge(s_silu, 1)
                modp = PS[5]
                for v, src in ((0, lambda t: rawo[:, t, :]), (1, lambda t: (ropeA, ropeB)[t // 2][:, t % 2, :])):
                    pe.wait_ge(s_wm[v], 16 if v == 0 else 16 * KT)
                    for f in range(KT):
                        for t in range(KT):
                            last = nc.tensor.matmul(modp[:, (v * KT + f) * B:(v * KT + f + 1) * B],
                                                    src(t)[:, f * P:(f + 1) * P], siluT[:, t, :],
                                                    start=t == 0, stop=t == KT - 1)
                last.then_inc(s_modp, 1)
                pe.wait_ge(s_const, 16)
                for b in range(B):
                    for f in range(KT):
                        m = b * KT + f
                        if f == 0:
                            pe.wait_ge(s_xn, (b + 1) * NT)
                        if m >= 3:
                            pe.wait_ge(s_ht, m - 2)
                        for t in range(NT):
                            src = xn[0][:, t, f * P:(f + 1) * P] if b == 0 else acc[:, NT + t, f * P:(f + 1) * P]
                            last = nc.tensor.transpose(PS[m % 3][:, t * P:(t + 1) * P], src, ident)
                        last.then_inc(s_xnT, 1)
                    pe.wait_ge(s_hlo, (b + 1) * KT)
                    if b == 0:
                        for k in range(ITEMS):
                            if k == 2:
                                pe.wait_ge(s_rope, 1)
                            if k == 3:
                                pe.wait_ge(s_vt, 1)
                            if k >= 4:
                                pe.wait_ge(s_rope, k - 2)
                            project(0, 0, k, (A_, B_)[k % 2])
                        turn_v(0, 0)
                pe.wait_ge(s_rope, ROPES - 1)
                project(0, 1, K_, A_)
                pe.wait_ge(s_vlo, 1)
                for h in range(R):
                    scores(0, 0, 0, h, first=True)

                def slots(g, b, i, last):
                    nonlocal items, vt_ahead
                    items, obank = ahead(g, b, i, last)
                    vt_ahead = not (last and b == 1)
                    nxt = following(g, b, i)
                    more = not (last and (b, i) == (B - 1, NT - 1))
                    for h in range(R):
                        if more:
                            scores(*nxt, h)
                        if h >= 1 and h - 1 <= i:
                            turn(g, b, i, h - 1)
                    if i == 3:
                        turn(g, b, i, 3)
                    if items:
                        bank_free(g, b, i, items[0][2])
                        project(*items[0])
                    values(g, b, i)
                    if len(items) > 1:
                        bank_free(g, b, i, items[1][2])
                        project(*items[1])
                    if items and items[0][2] == V_:
                        turn_v(items[0][0], items[0][1])
                    bank_free(g, b, i, "out")
                    output(g, b, i, obank)

                items, vt_ahead = [], True
                with pe.Fori(0, G - 1) as g:
                    for b in range(B):
                        for i in range(NT):
                            slots(g, b, i, False)
                for b in range(B):
                    for i in range(NT):
                        slots(G - 1, b, i, True)

            @main.scalar
            def _(act):
                def whi(g, k):
                    wait_raw(act, g, k)
                    nc.scalar.activation(wqkv["hi"][:, k, :, :], raw_item(k), ACT.Copy).then_inc(s_whi, 1)

                def qk_high(g, b, k):
                    r = rope_no(k)
                    act.wait_ge(s_rot, unit(g, b) * ROPES + (r + 1))
                    nc.scalar.activation(qkhi[:, b, r, :], ropeA[:, parity(b, r), :], ACT.Copy).then_inc(s_qkhi, 1)

                def v_copy(g, b):
                    act.wait_ge(s_proj, unit(g, b) * ITEMS + (V_ + 1))
                    nc.scalar.activation(vt[:, :], A_[:, :] if not prologue else B_[:, :], ACT.Identity,
                                         bias=bv_sb[:, bass.ds(g, 1)]).then_inc(s_vt, 1)

                def v_high(g, b):
                    act.wait_ge(s_vtr, unit(g, b) + 1)
                    nc.scalar.activation(vhi[:, b, :, :], pt_bank[1][:, :].rearrange("p (t d) -> p t d", t=NT),
                                         ACT.Copy).then_inc(s_vhi, 1)

                def exponent(g, b, i, h):
                    act.wait_ge(s_negmax, slot(g, b, i) * R + (h + 1))
                    nc.scalar.activation(prob[i % 2][:, h, 0:(i + 1) * P], s_bank[h][:, 0:(i + 1) * P], ACT.Exp,
                                         bias=negmax[:, i % 2, h:h + 1], scale=-1.0,
                                         accum_out=rowsum[:, i % 2, h:h + 1]).then_inc(s_exp, 1)

                def pt_high(g, b, i, j):
                    act.wait_ge(s_pt, pts(g, b, i) + (j + 1))
                    nc.scalar.activation(pthi[:, j, :], pt_bank[j % 2][:, :], ACT.Copy).then_inc(s_pthi, 1)

                act.wait_ge(s_c, 16)
                nc.scalar.activation(siluT[:, :, :], cT[:, :, :].rearrange("p b t -> p t b"), ACT.Exp, scale=-1.0)\
                    .then_inc(s_expc, 1)
                for k in range(ITEMS):
                    whi(0, k)
                act.wait_ge(s_bias, 48)
                prologue = True
                for b in range(B):
                    for f in range(KT):
                        m = b * KT + f
                        act.wait_ge(s_ht, m + 1)
                        nc.scalar.activation(hThi[:, f, b * S:(b + 1) * S], ht[m % 2][:, :], ACT.Copy)\
                            .then_inc(s_hhi, 1)
                    if b == 0:
                        qk_high(0, 0, K_)
                        v_copy(0, 0)
                        qk_high(0, 0, Q_)
                        for k in range(Q_ + 1, ITEMS):
                            qk_high(0, 0, k)
                        v_high(0, 0)
                prologue = False
                qk_high(0, 1, K_)
                for h in range(R):
                    exponent(0, 0, 0, h)

                def slots(g, b, i, last):
                    items, _ = ahead(g, b, i, last)
                    nxt = following(g, b, i)
                    more = not (last and (b, i) == (B - 1, NT - 1))
                    for h in range(R):
                        if more:
                            exponent(*nxt, h)
                        if h >= 1 and h - 1 <= i:
                            pt_high(g, b, i, h - 1)
                        if h == 1 and i in (1, 2) and not (last and b == 1):
                            late = ahead(g, b, i - 1, last)[0][1]
                            qk_high(late[0], late[1], late[2])
                    if i == 3:
                        pt_high(g, b, i, 3)
                    if (b, i) == (0, 0):
                        act.wait_ge(s_rawo, 16 * g + 16)
                        act.wait_ge(s_acc, g * SLOTS + 1)
                        for h in range(R):
                            nc.scalar.activation(wo["hi"][:, h, :], rawo[:, h, :], ACT.Copy).then_inc(s_wohi, 1)
                    if items and items[0][2] == V_:
                        v_copy(items[0][0], items[0][1])
                    act.wait_ge(s_ctx, slot(g, b, i) + 1)
                    nc.scalar.activation(ctxhi[:, :], ctx_bank[:, :], ACT.Copy).then_inc(s_ctxhi, 1)
                    if items and items[0][2] != V_:
                        qk_high(items[0][0], items[0][1], items[0][2])
                    if (b, i) in SPLIT_AT and not last:
                        k = SPLIT_AT[b, i]
                        act.wait_ge(s_proj, g * (2 * ITEMS) + (ITEMS + k + 1))
                        whi(g + 1, k)
                    if items and items[0][2] == V_:
                        v_high(items[0][0], items[0][1])

                with act.Fori(0, G - 1) as g:
                    for b in range(B):
                        for i in range(NT):
                            slots(g, b, i, False)
                for b in range(B):
                    for i in range(NT):
                        slots(G - 1, b, i, True)

            @main.gpsimd
            def _(pool):
                def wlow(g, k):
                    pool.wait_ge(s_whi, g * ITEMS + (k + 1))
                    nc.gpsimd.tensor_tensor(wqkv["lo"][:, k, :, :], raw_item(k),
                                            wqkv["hi"][:, k, :, :].bitcast(F32), ALU.subtract).then_inc(s_wlo, 1)

                def rotate(g, b, k):
                    r = rope_no(k)
                    q = parity(b, r)
                    pool.wait_ge(s_rope, unit(g, b) * ROPES + (r + 1))
                    nc.gpsimd.tensor_tensor(ropeA[:, q, :], ropeA[:, q, :], ropeB[:, q, :], ALU.add).then_inc(s_rot, 1)

                def qk_low(g, b, k):
                    r = rope_no(k)
                    pool.wait_ge(s_qkhi, unit(g, b) * ROPES + (r + 1))
                    nc.gpsimd.tensor_tensor(qklo[:, b, r, :], ropeA[:, parity(b, r), :],
                                            qkhi[:, b, r, :].bitcast(F32), ALU.subtract).then_inc(s_qklo, 1)

                def normalise(g, b, i, h):
                    if h % 2 == 0:
                        pool.wait_ge(s_rinv, slot(g, b, i) * 2 + (h // 2 + 1))
                    p = prob[i % 2][:, h, 0:(i + 1) * P]
                    nc.gpsimd.tensor_tensor(p, p, rinv[:, i % 2, h:h + 1].to_broadcast([P, (i + 1) * P]),
                                            ALU.mult).then_inc(s_prob, 1)

                def deviation(b):
                    pool.wait_ge(s_var, b + 1)
                    cols = slice(b * NT, (b + 1) * NT)
                    nc.gpsimd.tensor_tensor(rstd[:, cols], var[:, cols], half[:, cols], ALU.pow).then_inc(s_rstd, 1)

                nc.gpsimd.memset(half[:, :], -0.5).then_inc(s_half, 1)
                pool.wait_ge(s_half, 1)
                deviation(0)
                wlow(0, K_)
                for b in range(B):
                    if b == 1:
                        deviation(1)
                    for f in range(KT):
                        m = b * KT + f
                        pool.wait_ge(s_hhi, m + 1)
                        nc.gpsimd.tensor_tensor(hTlo[:, f, b * S:(b + 1) * S], ht[m % 2][:, :],
                                                hThi[:, f, b * S:(b + 1) * S].bitcast(F32), ALU.subtract)\
                            .then_inc(s_hlo, 1)
                    if b == 0:
                        for k in range(V_, ITEMS):
                            wlow(0, k)
                            if k == V_:
                                continue
                            prev = K_ if k == Q_ else k - 1
                            rotate(0, 0, prev)
                            qk_low(0, 0, prev)
                        rotate(0, 0, ITEMS - 1)
                        qk_low(0, 0, ITEMS - 1)
                rotate(0, 1, K_)
                qk_low(0, 1, K_)
                for h in range(R):
                    normalise(0, 0, 0, h)

                def slots(g, b, i, last):
                    items, _ = ahead(g, b, i, last)
                    nxt = following(g, b, i)
                    more = not (last and (b, i) == (B - 1, NT - 1))
                    late = i in (1, 2) and not (last and b == 1)
                    for h in range(R):
                        if more:
                            normalise(*nxt, h)
                        if h == 1 and late:
                            item = ahead(g, b, i - 1, last)[0][1]
                            qk_low(item[0], item[1], item[2])
                    if items and items[0][2] != V_:
                        rotate(items[0][0], items[0][1], items[0][2])
                        qk_low(items[0][0], items[0][1], items[0][2])
                    if len(items) > 1:
                        rotate(items[1][0], items[1][1], items[1][2])
                    if (b, i) in SPLIT_AT and not last:
                        wlow(g + 1, SPLIT_AT[b, i])

                with pool.Fori(0, G - 1) as g:
                    for b in range(B):
                        for i in range(NT):
                            slots(g, b, i, False)
                for b in range(B):
                    for i in range(NT):
                        slots(G - 1, b, i, True)

            @main.vector
            def _(dve):
                chain = [0]

                def link(ins):
                    chain[0] += 1
                    ins.then_inc(s_dve, 1)
                    dve.wait_ge(s_dve, chain[0])

                def rope(g, b, k, bank):
                    r = rope_no(k)
                    q = parity(b, r)
                    item = unit(g, b) * ROPES + r
                    if not (isinstance(g, int) and g == 0 and b == 0 and r < 2):
                        dve.wait_ge(s_qklo, item - 1)
                    dve.wait_ge(s_proj, unit(g, b) * ITEMS + (k + 1))
                    if k == K_:
                        lo, hi = bk_sb[0:64, bass.ds(g, 1)], bk_sb[64:128, bass.ds(g, 1)]
                        both = bk_sb[:, bass.ds(g, 1)]
                    else:
                        at = bass.ds(g * R + (k - Q_), 1)
                        lo, hi, both = bq_sb[0:64, at], bq_sb[64:128, at], bq_sb[:, at]
                    nc.vector.scalar_tensor_tensor(out=ropeA[:, q, :], in0=bank[:, :], scalar=both, in1=cos,
                                                   op0=ALU.add, op1=ALU.mult)
                    nc.vector.scalar_tensor_tensor(out=ropeB[0:64, q, :], in0=bank[64:128, :], scalar=hi,
                                                   in1=sin[64:128, :], op0=ALU.add, op1=ALU.mult)
                    nc.vector.scalar_tensor_tensor(out=ropeB[64:128, q, :], in0=bank[0:64, :], scalar=lo,
                                                   in1=sin[0:64, :], op0=ALU.add, op1=ALU.mult).then_inc(s_rope, 1)

                def v_low(g, b):
                    dve.wait_ge(s_vhi, unit(g, b) + 1)
                    nc.vector.tensor_tensor(vlo[:, b, :, :], pt_bank[1][:, :].rearrange("p (t d) -> p t d", t=NT),
                                            vhi[:, b, :, :].bitcast(F32), ALU.subtract).then_inc(s_vlo, 1)

                def maximum(g, b, i, h):
                    w = (i + 1) * P
                    dve.wait_ge(s_scores, slot(g, b, i) * R + (h + 1))
                    dve.nop(nofuse=True)
                    nc.vector.tensor_tensor_reduce(out=s_bank[h][:, 0:w], in0=s_bank[h][:, 0:w], in1=mask[:, S - w:S],
                                                   scale=-SCALE, scalar=3.0e38, op0=ALU.add, op1=ALU.min,
                                                   accum_out=negmax[:, i % 2, h:h + 1]).then_inc(s_negmax, 1)

                def invert(g, b, i, pair):
                    dve.wait_ge(s_exp, slot(g, b, i) * R + (2 * pair + 2))
                    nc.vector.reciprocal(rinv[:, i % 2, 2 * pair:2 * pair + 2],
                                         rowsum[:, i % 2, 2 * pair:2 * pair + 2]).then_inc(s_rinv, 1)

                def pt_low(g, b, i, j):
                    dve.wait_ge(s_pthi, pts(g, b, i) + (j + 1))
                    nc.vector.tensor_tensor(ptlo[:, j, :], pt_bank[j % 2][:, :], pthi[:, j, :].bitcast(F32),
                                            ALU.subtract).then_inc(s_ptlo, 1)

                dve.wait_ge(s_expc, 1)
                link(nc.vector.tensor_scalar(siluT[:, :, :], siluT[:, :, :], 1.0, None, ALU.add))
                link(nc.vector.reciprocal(siluT[:, :, :], siluT[:, :, :]))
                nc.vector.tensor_tensor(siluT[:, :, :], siluT[:, :, :], cT[:, :, :].rearrange("p b t -> p t b"),
                                        ALU.mult).then_inc(s_silu, 1)

                def layer_norm(b):
                    dve.wait_ge(s_x[b], 16)
                    tiles = range(b * NT, (b + 1) * NT)
                    for t in tiles:
                        last = nc.vector.bn_stats(stats[:, t, :], acc[:, t, :])
                    link(last)
                    for t in tiles:
                        last = nc.vector.bn_aggr(mv[:, t, :], stats[:, t, :])
                    link(last)
                    nc.vector.tensor_scalar(var[:, b * NT:(b + 1) * NT], mv[:, b * NT:(b + 1) * NT, 1],
                                            EPS, None, ALU.add).then_inc(s_var, 1)
                    dve.wait_ge(s_rstd, b + 1)
                    for t in tiles:
                        dst = xn[0][:, t, :] if b == 0 else acc[:, t, :]
                        nc.vector.tensor_scalar(dst, acc[:, t, :], mv[:, t, 0:1], rstd[:, t:t + 1],
                                                ALU.subtract, ALU.mult).then_inc(s_xn, 1)

                layer_norm(0)
                dve.wait_ge(s_modp, 1)
                modp = PS[5]
                nc.vector.tensor_copy(modT[:, 0, :, :].rearrange("p f b -> p (f b)"), modp[:, 0:KT * B])
                link(nc.vector.tensor_scalar(modT[:, 1, :, :].rearrange("p f b -> p (f b)"), modp[:, KT * B:2 * KT * B],
                                             1.0, None, ALU.add))
                dve.wait_ge(s_bias, 48)
                dve.wait_ge(s_const, 16)
                for b in range(B):
                    if b == 1:
                        layer_norm(1)
                    for f in range(KT):
                        m = b * KT + f
                        dve.wait_ge(s_xnT, m + 1)
                        if m >= 2:
                            dve.wait_ge(s_hlo, m - 1)
                        nc.vector.tensor_scalar(ht[m % 2][:, :], PS[m % 3][:, :], modT[:, 1, f, b:b + 1],
                                                modT[:, 0, f, b:b + 1], ALU.mult, ALU.add).then_inc(s_ht, 1)
                    if b == 0:
                        rope(0, 0, K_, A_)
                        rope(0, 0, Q_, A_)
                        for k in range(Q_ + 1, ITEMS):
                            rope(0, 0, k, (A_, B_)[k % 2])
                        v_low(0, 0)
                rope(0, 1, K_, A_)
                for h in range(R):
                    maximum(0, 0, 0, h)
                    if h % 2:
                        invert(0, 0, 0, h // 2)
                dve.wait_ge(s_bo, 16 * B * NT)
                dve.sem_inc(s_acc, 1)

                def slots(g, b, i, last):
                    items, obank = ahead(g, b, i, last)
                    nxt = following(g, b, i)
                    more = not (last and (b, i) == (B - 1, NT - 1))
                    for h in range(R):
                        if more:
                            maximum(*nxt, h)
                        if h >= 1 and h - 1 <= i:
                            pt_low(g, b, i, h - 1)
                        if more and h == 2:
                            invert(*nxt, 0)
                    if i == 3:
                        pt_low(g, b, i, 3)
                    if more:
                        invert(*nxt, 1)
                    if items and items[0][2] != V_:
                        rope(*items[0])
                    if (b, i) == (0, 0):
                        for h in range(R):
                            dve.wait_ge(s_wohi, g * R + (h + 1))
                            nc.vector.tensor_tensor(wo["lo"][:, h, :], rawo[:, h, :], wo["hi"][:, h, :].bitcast(F32),
                                                    ALU.subtract).then_inc(s_wolo, 1)
                    dve.wait_ge(s_ctxhi, slot(g, b, i) + 1)
                    nc.vector.tensor_tensor(ctxlo[:, :], ctx_bank[:, :], ctxhi[:, :].bitcast(F32),
                                            ALU.subtract).then_inc(s_ctxlo, 1)
                    if len(items) > 1:
                        rope(*items[1])
                    if items and items[0][2] == V_:
                        v_low(items[0][0], items[0][1])
                    dve.wait_ge(s_o, slot(g, b, i) + 1)
                    a = acc[:, b * NT + i, :]
                    nc.vector.tensor_tensor(a, obank[:, :], a, ALU.add).then_inc(s_acc, 1)

                with dve.Fori(0, G - 1) as g:
                    for b in range(B):
                        for i in range(NT):
                            slots(g, b, i, False)
                for b in range(B):
                    for i in range(NT):
                        slots(G - 1, b, i, True)

        with ExitStack() as ffn:
            def tb(name, shape, dt=F32):
                return sb(name, shape, dt, ffn)

            NM = B * NT
            x2 = tb("x2", [P, NM, HID])
            wmt = [tb(f"wmt{v}", [P, KT, HID]) for v in range(2, 6)]
            baser = tb("baser", [P, KT, HID])
            base = {hl: tb(f"base{hl}", [P, KT, HID], F32R) for hl in ("hi", "lo")}
            lar = tb("lar", [P, KT, LORA_PAD])
            la = {hl: tb(f"la{hl}", [P, KT, LORA_PAD], F32R) for hl in ("hi", "lo")}
            lbr = tb("lbr", [P, HID])
            lb = {hl: tb(f"lb{hl}", [P, HID], F32R) for hl in ("hi", "lo")}
            gw = tb("gw", [P, KT, E])
            bb = tb("bb", [P, HID])
            io8 = tb("io8", [P, E])
            ncol = tb("ncol", [P, KT, P])
            gbc = tb("gbc", [P, 2, B, HID])
            xn2 = tb("xn2", [P, 2, HID])
            h2 = tb("h2", [P, KT, P * 2])
            h2hi = tb("h2hi", [P, 2, KT, P], F32R)
            h2lo = tb("h2lo", [P, 2, KT, P], F32R)
            top = tb("top", [P, 8])
            topi = tb("topi", [P, 8], U32)
            logit = tb("logit", [P, E])
            small = tb("small", [P, 8])
            oneh = tb("oneh", [P, 2, E])
            lw = tb("lw", [P, 2, P])
            lwhi = tb("lwhi", [P, 2, P], F32R)
            lwlo = tb("lwlo", [P, 2, P], F32R)
            neg = tb("neg", [P, 2 * KT * B])
            t_x, t_wm, t_base, t_la, t_lb, t_misc = sem("t_x"), [sem(f"t_wm{v}") for v in range(4)], sem("t_base"), sem("t_la"), sem("t_lb"), sem("t_misc")
            t_modp, t_ncol, t_bc, t_bcd = sem("t_modp"), sem("t_ncol"), sem("t_bc"), sem("t_bcd")
            t_whi, t_wlo = sem("t_whi"), sem("t_wlo")
            t_xn, t_xT, t_h, t_hhi, t_hlo = sem("t_xn"), sem("t_xT"), sem("t_h"), sem("t_hhi"), sem("t_hlo")
            t_gate, t_low, t_diff, t_e, t_lw, t_lwT, t_lwhi, t_lwlo = (sem("t_gate"), sem("t_low"), sem("t_diff"),
                sem("t_e"), sem("t_lw"), sem("t_lwT"), sem("t_lwhi"), sem("t_lwlo"))
            t_y, t_out, t_done, t_dve = sem("t_y"), sem("t_out"), sem("t_done"), sem("t_dve")
            t_var, t_rstd = sem("t_var"), sem("t_rstd")

            tail = ffn.enter_context(nc.Block())
            mod_bank, bc_bank, xT_bank, low_bank, y_bank = PS[0], PS[1], [PS[2], PS[3]], [PS[4], PS[5]], [PS[6], PS[7]]

            @tail.sync
            def _(sp):
                wms = wmod.rearrange("(p t) n -> p t n", t=KT)
                for v in range(4):
                    sp.dma_start(wmt[v][:, :, :], wms[:, :, (v + 2) * HID:(v + 3) * HID]).then_inc(t_wm[v], 16)
                    if v == 0:
                        sp.dma_start(x2[:, :, :].rearrange("p (b t) n -> p b t n", b=B),
                                     x.rearrange("b (t p) n -> p b t n", p=P)).then_inc(t_x, 16)
                sp.dma_start(lar[:, :, :], loraAT.rearrange("(t p) n -> p t n", p=P)).then_inc(t_la, 16)
                sp.dma_start(gw[:, :, :], gateT.rearrange("(t p) n -> p t n", p=P)).then_inc(t_misc, 16)
                sp.dma_start(bb[:, :], base_b.broadcast_to([P, HID])).then_inc(t_misc, 16)
                sp.dma_start(io8[:, :], iota8.broadcast_to([P, E])).then_inc(t_misc, 16)
                sp.dma_start(baser[:, :, :], baseT.rearrange("(t p) n -> p t n", p=P)).then_inc(t_base, 16)
                sp.dma_start(lbr[:, :], loraB).then_inc(t_lb, 16)
                ov = out.rearrange("b (t p) n -> (b t) p n", p=P)
                for m in range(NM):
                    sp.wait_ge(t_out, m + 1)
                    sp.dma_start(ov[m], x2[:, m, :]).then_inc(t_done, 16)
                sp.wait_ge(t_done, 16 * NM)

            @tail.tensor
            def _(pe):
                def three(out, whi, wlo, xhi, xlo, start, stop):
                    nc.tensor.matmul(out, whi, xhi, start=start, stop=False)
                    nc.tensor.matmul(out, whi, xlo, start=False, stop=False)
                    return nc.tensor.matmul(out, wlo, xhi, start=False, stop=stop)

                for v in range(4):
                    pe.wait_ge(t_wm[v], 16)
                    for f in range(KT):
                        for t in range(KT):
                            last = nc.tensor.matmul(mod_bank[:, (v * KT + f) * B:(v * KT + f + 1) * B],
                                                    wmt[v][:, t, f * P:(f + 1) * P], siluT[:, t, :],
                                                    start=t == 0, stop=t == KT - 1)
                last.then_inc(t_modp, 1)
                for k in range(2 * B):
                    pe.wait_ge(t_ncol, k + 1)
                    if k:
                        pe.wait_ge(t_bcd, k)
                    for f in range(KT):
                        last = nc.tensor.matmul(bc_bank[:, f * P:(f + 1) * P], ncol[:, f, :], ident,
                                                start=True, stop=True)
                    last.then_inc(t_bc, 1)

                def front(m):
                    pe.wait_ge(t_xn, m + 1)
                    if m >= 2:
                        pe.wait_ge(t_h, m - 1)
                    for f in range(KT):
                        last = nc.tensor.transpose(xT_bank[m % 2][:, f * P:(f + 1) * P],
                                                   xn2[:, m % 2, f * P:(f + 1) * P], ident)
                    last.then_inc(t_xT, 1)

                def back(m):
                    pe.wait_ge(t_hlo, m + 1)
                    if m == 0:
                        pe.wait_ge(t_misc, 48)
                        pe.wait_ge(t_wlo, 1)
                    if m >= 2:
                        pe.wait_ge(t_lw, m - 1)
                        pe.wait_ge(t_lwlo, m - 1)
                    low = low_bank[m % 2]
                    for t in range(KT):
                        last = nc.tensor.matmul(low[:, 256:256 + E], h2[:, t, (m % 2) * P:(m % 2 + 1) * P], gw[:, t, :],
                                                start=t == 0, stop=t == KT - 1)
                    last.then_inc(t_gate, 1)
                    for t in range(KT):
                        last = three(low[:, 0:256], h2hi[:, m % 2, t, :], h2lo[:, m % 2, t, :], la["hi"][:, t, :],
                                     la["lo"][:, t, :], t == 0, t == KT - 1)
                    last.then_inc(t_low, 1)
                    if m == 0:
                        pe.wait_ge(t_wlo, 3)
                    if m >= 2:
                        pe.wait_ge(t_out, m - 1)
                    y = y_bank[m % 2]
                    for t in range(KT):
                        three(y[:, :], h2hi[:, m % 2, t, :], h2lo[:, m % 2, t, :], base["hi"][:, t, :],
                              base["lo"][:, t, :], t == 0, False)
                    pe.wait_ge(t_lw, m + 1)
                    nc.tensor.transpose(low[:, 384:512], lw[:, m % 2, :], ident).then_inc(t_lwT, 1)
                    pe.wait_ge(t_lwlo, m + 1)
                    three(y[:, :], lwhi[:, m % 2, :], lwlo[:, m % 2, :], lb["hi"][:, :], lb["lo"][:, :], False, True)\
                        .then_inc(t_y, 1)

                front(0)
                for m in range(NM):
                    if m + 1 < NM:
                        front(m + 1)
                    back(m)

            @tail.scalar
            def _(act):
                act.wait_ge(t_la, 16)
                nc.scalar.activation(la["hi"][:, :, :], lar[:, :, :], ACT.Copy).then_inc(t_whi, 1)
                act.wait_ge(t_base, 16)
                nc.scalar.activation(base["hi"][:, :, :], baser[:, :, :], ACT.Copy).then_inc(t_whi, 1)
                act.wait_ge(t_lb, 16)
                nc.scalar.activation(lb["hi"][:, :], lbr[:, :], ACT.Copy).then_inc(t_whi, 1)

                def h_high(m):
                    act.wait_ge(t_h, m + 1)
                    if m >= 2:
                        act.wait_ge(t_y, m - 1)
                    nc.scalar.activation(h2hi[:, m % 2, :, :], h2[:, :, (m % 2) * P:(m % 2 + 1) * P], ACT.Copy)\
                        .then_inc(t_hhi, 1)

                h_high(0)
                for m in range(NM):
                    if m + 1 < NM:
                        h_high(m + 1)
                    act.wait_ge(t_diff, m + 1)
                    nc.scalar.activation(small[:, 1:2], small[:, 0:1], ACT.Exp).then_inc(t_e, 1)
                    act.wait_ge(t_lwT, m + 1)
                    nc.scalar.activation(lwhi[:, m % 2, :], low_bank[m % 2][:, 384:512], ACT.Copy).then_inc(t_lwhi, 1)

            @tail.gpsimd
            def _(pool):
                for k, (dst, hi, src) in enumerate(((la["lo"], la["hi"], lar), (base["lo"], base["hi"], baser))):
                    pool.wait_ge(t_whi, k + 1)
                    nc.gpsimd.tensor_tensor(dst[:, :, :], src[:, :, :], hi[:, :, :].bitcast(F32), ALU.subtract)\
                        .then_inc(t_wlo, 1)
                pool.wait_ge(t_whi, 3)
                nc.gpsimd.tensor_tensor(lb["lo"][:, :], lbr[:, :], lb["hi"][:, :].bitcast(F32), ALU.subtract)\
                    .then_inc(t_wlo, 1)
                for m in range(NM):
                    pool.wait_ge(t_var, m + 1)
                    nc.gpsimd.tensor_tensor(rstd[:, m:m + 1], var[:, m:m + 1], half[:, m:m + 1], ALU.pow)\
                        .then_inc(t_rstd, 1)

            @tail.vector
            def _(dve):
                chain = [0]

                def link(ins):
                    chain[0] += 1
                    ins.then_inc(t_dve, 1)
                    dve.wait_ge(t_dve, chain[0])

                dve.wait_ge(t_modp, 1)
                link(nc.vector.tensor_copy(modT[:, 2:6, :, :].rearrange("p v f b -> p (v f b)"), mod_bank[:, 0:4 * KT * B]))
                link(nc.vector.tensor_scalar(modT[:, 4, :, :], modT[:, 4, :, :], 1.0, None, ALU.add))
                for v in (2, 5):
                    s = neg[:, 0:KT * B].rearrange("p (f b) -> p f b", f=KT)
                    n = neg[:, KT * B:2 * KT * B].rearrange("p (f b) -> p f b", f=KT)
                    link(nc.vector.tensor_scalar(s, modT[:, v, :, :], 0.0, 2.0, ALU.is_ge, ALU.mult))
                    link(nc.vector.tensor_scalar(s, s, -1.0, None, ALU.add))
                    link(nc.vector.tensor_tensor(n, s, modT[:, v, :, :], ALU.mult))
                    link(nc.vector.tensor_scalar(n, n, 0.25, None, ALU.max))
                    link(nc.vector.tensor_tensor(modT[:, v, :, :], s, n, ALU.mult))
                k = 0
                for q, v in enumerate((2, 5)):
                    for b in range(B):
                        if k:
                            dve.wait_ge(t_bc, k)
                        nc.vector.tensor_copy(ncol[:, :, :], modT[:, v, :, b:b + 1].to_broadcast([P, KT, P]))\
                            .then_inc(t_ncol, 1)
                        k += 1
                        dve.wait_ge(t_bc, k)
                        nc.vector.tensor_copy(gbc[:, q, b, :], bc_bank[:, :]).then_inc(t_bcd, 1)
                dve.wait_ge(t_bcd, 2 * B)
                dve.wait_ge(t_misc, 48)
                dve.wait_ge(t_x, 16)

                def front(m):
                    b = m // NT
                    a = acc[:, m, :]
                    link(nc.vector.tensor_tensor(a, a, gbc[:, 0, b, :], ALU.mult))
                    link(nc.vector.tensor_tensor(a, a, x2[:, m, :], ALU.add))
                    link(nc.vector.bn_stats(stats[:, m, :], a))
                    link(nc.vector.bn_aggr(mv[:, m, :], stats[:, m, :]))
                    nc.vector.tensor_scalar(var[:, m:m + 1], mv[:, m, 1:2], EPS, None, ALU.add).then_inc(t_var, 1)
                    dve.wait_ge(t_rstd, m + 1)
                    if m >= 2:
                        dve.wait_ge(t_xT, m - 1)
                    nc.vector.tensor_scalar(xn2[:, m % 2, :], a, mv[:, m, 0:1], rstd[:, m:m + 1],
                                            ALU.subtract, ALU.mult).then_inc(t_xn, 1)

                def modulate(m):
                    b = m // NT
                    dve.wait_ge(t_xT, m + 1)
                    if m >= 2:
                        dve.wait_ge(t_gate, m - 1)
                    for f in range(KT):
                        last = nc.vector.tensor_scalar(h2[:, f, (m % 2) * P:(m % 2 + 1) * P],
                                                       xT_bank[m % 2][:, f * P:(f + 1) * P],
                                                       modT[:, 4, f, b:b + 1], modT[:, 3, f, b:b + 1], ALU.mult, ALU.add)
                    last.then_inc(t_h, 1)
                    dve.wait_ge(t_hhi, m + 1)
                    nc.vector.tensor_tensor(h2lo[:, m % 2, :, :], h2[:, :, (m % 2) * P:(m % 2 + 1) * P],
                                            h2hi[:, m % 2, :, :].bitcast(F32), ALU.subtract).then_inc(t_hlo, 1)

                def route(m):
                    low = low_bank[m % 2]
                    dve.wait_ge(t_low, m + 1)
                    link(nc.vector.tensor_copy(logit[:, :], low[:, 256:256 + E]))
                    link(nc.vector.max(top[:, :], logit[:, :]))
                    link(nc.vector.max_index(topi[:, :], top[:, :], logit[:, :]))
                    link(nc.vector.tensor_copy(small[:, 4:6], topi[:, 0:2]))
                    nc.vector.tensor_tensor(small[:, 0:1], top[:, 1:2], top[:, 0:1], ALU.subtract).then_inc(t_diff, 1)
                    dve.wait_ge(t_e, m + 1)
                    link(nc.vector.tensor_scalar(small[:, 2:3], small[:, 1:2], 1.0, 0.5, ALU.add, ALU.mult))
                    link(nc.vector.reciprocal(small[:, 2:3], small[:, 2:3]))
                    link(nc.vector.tensor_tensor(small[:, 3:4], small[:, 1:2], small[:, 2:3], ALU.mult))
                    for k in range(2):
                        last = nc.vector.tensor_scalar(oneh[:, k, :], io8[:, :], small[:, 4 + k:5 + k],
                                                       small[:, 2 + k:3 + k], ALU.is_equal, ALU.mult)
                    link(last)
                    link(nc.vector.tensor_tensor(oneh[:, 0, :], oneh[:, 0, :], oneh[:, 1, :], ALU.add))
                    if m >= 2:
                        dve.wait_ge(t_lwT, m - 1)
                    nc.vector.tensor_tensor(lw[:, m % 2, :].rearrange("p (e r) -> p e r", e=E),
                                            low[:, 0:P].rearrange("p (e r) -> p e r", e=E),
                                            oneh[:, 0, :].unsqueeze(2).to_broadcast([P, E, RANK]), ALU.mult)\
                        .then_inc(t_lw, 1)

                def finish(m):
                    b = m // NT
                    dve.wait_ge(t_lwhi, m + 1)
                    nc.vector.tensor_tensor(lwlo[:, m % 2, :], low_bank[m % 2][:, 384:512],
                                            lwhi[:, m % 2, :].bitcast(F32), ALU.subtract).then_inc(t_lwlo, 1)
                    dve.wait_ge(t_y, m + 1)
                    o = x2[:, m, :]
                    link(nc.vector.tensor_tensor(o, y_bank[m % 2][:, :], bb[:, :], ALU.add))
                    link(nc.vector.tensor_tensor(o, o, gbc[:, 1, b, :], ALU.mult))
                    nc.vector.tensor_tensor(o, o, acc[:, m, :], ALU.add).then_inc(t_out, 1)

                front(0)
                modulate(0)
                for m in range(NM):
                    if m + 1 < NM:
                        front(m + 1)
                        modulate(m + 1)
                    route(m)
                    finish(m)


def kernel(**inputs):
    import numpy as np
    import concourse.bacc as bacc
    from concourse.bass_utils import run_bass_kernel_spmd

    a = {k.replace("L0_", "", 1): np.asarray(v) for k, v in inputs.items()}
    half = D // 2
    inv_freq = (np.float32(1.0) / np.float32(10000.0) ** (np.arange(half, dtype=np.float32) / np.float32(half))).astype(np.float32)
    ang = (inv_freq[:, None] * np.arange(S, dtype=np.float32)[None, :]).astype(np.float32)
    cos, sin = np.cos(ang).astype(np.float32), np.sin(ang).astype(np.float32)
    consts = np.zeros((P, 3 * S + P), np.float32)
    consts[:, 0:S] = np.concatenate([cos, cos])
    consts[:, S:2 * S] = np.concatenate([sin, -sin])
    consts[:, 3 * S - P:3 * S] = np.where(np.arange(P)[None, :] > np.arange(P)[:, None], np.float32(MASKED), 0)
    consts[:, 3 * S:] = np.eye(P, dtype=np.float32)

    def by_group(w, n):
        return w.reshape(KT, P, G, n).transpose(2, 1, 0, 3)

    lora_a = np.zeros((HID, LORA_PAD), np.float32)
    lora_a[:, 0:E * RANK] = a["ffn_lora_A"].reshape(E * RANK, HID).T
    arrays = {
        "x": a["attn_hidden_states"],
        "Wq": by_group(a["attn_Wq"], R * D), "Wk": by_group(a["attn_Wk"], D), "Wv": by_group(a["attn_Wv"], D),
        "Wo": a["attn_Wo"].reshape(G, R, D, HID).transpose(0, 2, 1, 3),
        "bq": a["attn_bq"].reshape(H, D).T, "bk": a["attn_bk"].reshape(G, D).T, "bv": a["attn_bv"].reshape(G, D).T,
        "bo": a["attn_bo"].reshape(1, HID),
        "gateT": a["ffn_gate_w"].T, "baseT": a["ffn_base_w"].T, "base_b": a["ffn_base_b"].reshape(1, HID),
        "loraAT": lora_a, "loraB": a["ffn_lora_B"].transpose(0, 2, 1).reshape(E * RANK, HID),
        "c": a["c"], "wmod": a["wmod"], "consts": consts, "iota8": np.arange(E, dtype=np.float32).reshape(1, E),
    }
    nc = bacc.Bacc("TRN2", target_bir_lowering=False, num_devices=1)
    data, args = {}, []
    for name, v in arrays.items():
        v = np.ascontiguousarray(v)
        data[f"in_{name}"] = v
        args.append(nc.dram_tensor(f"in_{name}", v.shape, mybir.dt.from_np(v.dtype), kind="ExternalInput").ap())
    out = nc.dram_tensor("out", (B, S, HID), F32, kind="ExternalOutput").ap()
    adaln_block(nc, *args, out)
    r = run_bass_kernel_spmd(nc, [data], core_ids=[0])
    return r.results[0]["out"]
```

```python
from contextlib import ExitStack

import concourse.bass as bass
from concourse import mybir

B, S, HID = 2, 512, 512
H, G, D = 32, 8, 128
R = H // G
P = 128
KT = HID // P
NT = S // P
E, RANK = 8, 16
EPS = 1e-5
SCALE = float(D) ** -0.5
MASKED = -(2.0 ** 127)
SLOTS = B * NT
TRI = [0, 1, 3, 6, 10]
ITEMS = 2 + R
ROPES = 1 + R
K_, V_ = 0, 2
QS = [1, 3, 4, 5]
LORA_PAD = 256
NM = B * NT
VECTORS = {0: [2], 1: [3], 2: [4, 5]}
SPLIT_AT = {(0, 0): [0, 1], (0, 3): [2], (1, 0): [3, 4, 5]}
FILLS = [(1, 1, 2), (1, 1, 2), (2, 2, 2, 2), (2, 1, 1, 2, 2)]
WO_ORDER = [0, 3, 1, 2]
WO_POOL = 1

F32 = mybir.dt.float32
F32R = mybir.dt.float32r
U32 = mybir.dt.uint32
ALU = mybir.AluOpType
ACT = mybir.ActivationFunctionType


def adaln_block(nc, x, Wq, Wk, Wv, Wo, bq, bk, bv, bo, gateT, baseT, base_b, loraAT, loraB, c, wmod,
                consts, iota8, out):
    ctx = ExitStack()
    with ctx:
        def sb(name, shape, dt=F32, stack=ctx):
            return stack.enter_context(nc.sbuf_tensor(name, shape, dt))

        def sem(name):
            return ctx.enter_context(nc.semaphore(name))

        const = sb("const", [P, 3 * S + P])
        cos = const[:, 0:S]
        sin = const[:, S:2 * S]
        mask = const[:, 2 * S:3 * S]
        ident = const[:, 3 * S:3 * S + P]
        acc = sb("acc", [P, B * NT, HID])
        cT = sb("cT", [P, B, KT])
        siluT = sb("siluT", [P, KT, B])
        modT = sb("modT", [P, 6, KT, B])
        stats = sb("stats", [P, B * NT, 6])
        mv = sb("mv", [P, B * NT, 2])
        var = sb("var", [P, B * NT])
        rstd = sb("rstd", [P, B * NT])
        half = sb("half", [P, B * NT])
        bq_sb = sb("bq_sb", [P, H])
        bk_sb = sb("bk_sb", [P, G])
        bv_sb = sb("bv_sb", [P, G])
        negmax = sb("negmax", [P, 2, R])
        rowsum = sb("rowsum", [P, 2, R])
        rinv = sb("rinv", [P, 2, R])
        gw = sb("gw", [P, KT, E])
        io8 = sb("io8", [P, E])
        top = sb("top", [P, 8])
        topi = sb("topi", [P, 8], U32)
        logit = sb("logit", [P, E])
        small = sb("small", [P, 8])
        oneh = sb("oneh", [P, 2, E])
        neg = sb("neg", [P, 2, KT * B])
        PS = [ctx.enter_context(nc.psum_tensor(f"bank{k}", [P, 512], F32)) for k in range(8)]
        s_bank = [PS[0], PS[1], PS[2], PS[0]]
        pt_bank = [PS[3], PS[4]]
        ctx_bank = PS[5]
        A_, B_ = PS[6], PS[7]

        s_x = [sem(f"s_x{b}") for b in range(B)]
        s_ident = sem("s_ident")
        s_const, s_c, s_bias, s_bo = sem("s_const"), sem("s_c"), sem("s_bias"), sem("s_bo")
        s_wm = [sem(f"s_wm{k}") for k in range(2)]
        s_rawk, s_rawv, s_rawq, s_rawo = sem("s_rawk"), sem("s_rawv"), sem("s_rawq"), sem("s_rawo")
        s_expc, s_silu = sem("s_expc"), sem("s_silu")
        s_modp, s_mod = sem("s_modp"), sem("s_mod")
        s_half, s_var, s_rstd = sem("s_half"), sem("s_var"), sem("s_rstd")
        s_dve = sem("s_dve")
        s_xn, s_xnT, s_ht, s_hhi, s_hlo = sem("s_xn"), sem("s_xnT"), sem("s_ht"), sem("s_hhi"), sem("s_hlo")
        s_whi, s_wlo, s_wohi, s_wolo = sem("s_whi"), sem("s_wlo"), sem("s_wohi"), sem("s_wolo")
        s_wolo_pool = sem("s_wolo_pool")
        s_proj, s_rope, s_rot, s_qkhi, s_qklo = sem("s_proj"), sem("s_rope"), sem("s_rot"), sem("s_qkhi"), sem("s_qklo")
        s_vt, s_vtr, s_vhi, s_vlo = sem("s_vt"), sem("s_vtr"), sem("s_vhi"), sem("s_vlo")
        s_scores, s_negmax, s_exp, s_rinv, s_prob = sem("s_scores"), sem("s_negmax"), sem("s_exp"), sem("s_rinv"), sem("s_prob")
        s_pt, s_pthi, s_ptlo = sem("s_pt"), sem("s_pthi"), sem("s_ptlo")
        s_ctx, s_ctxhi, s_ctxlo, s_o, s_acc = sem("s_ctx"), sem("s_ctxhi"), sem("s_ctxlo"), sem("s_o"), sem("s_acc")

        t_x = [sem(f"t_x{m}") for m in range(NM)]
        t_wm = [sem(f"t_wm{v}") for v in range(2, 6)]
        t_base, t_la, t_lb, t_gw, t_bb = sem("t_base"), sem("t_la"), sem("t_lb"), sem("t_gw"), sem("t_bb")
        t_modp, t_mod, t_ncol, t_bc, t_bcd = sem("t_modp"), sem("t_mod"), sem("t_ncol"), sem("t_bc"), sem("t_bcd")
        t_lahi, t_lalo, t_lbhi, t_lblo = sem("t_lahi"), sem("t_lalo"), sem("t_lbhi"), sem("t_lblo")
        t_basehi, t_baselo, t_gbb = sem("t_basehi"), sem("t_baselo"), sem("t_gbb")
        t_pool = sem("t_pool")
        t_gated, t_var, t_rstd, t_xn, t_xT = sem("t_gated"), sem("t_var"), sem("t_rstd"), sem("t_xn"), sem("t_xT")
        t_h, t_hhi, t_hlo, t_gate, t_low = sem("t_h"), sem("t_hhi"), sem("t_hlo"), sem("t_gate"), sem("t_low")
        t_diff, t_e, t_lw, t_lwT, t_lwhi, t_lwlo = (sem("t_diff"), sem("t_e"), sem("t_lw"), sem("t_lwT"),
                                                    sem("t_lwhi"), sem("t_lwlo"))
        t_y, t_prod, t_out, t_outlast, t_done = sem("t_y"), sem("t_prod"), sem("t_out"), sem("t_outlast"), sem("t_done")

        with ExitStack() as attn:
            hThi = sb("hThi", [P, KT, B * S], F32R, attn)
            hTlo = sb("hTlo", [P, KT, B * S], F32R, attn)
            wqkv = {hl: sb(f"wqkv{hl}", [P, ITEMS, KT, P], F32R, attn) for hl in ("hi", "lo")}
            wo = {hl: sb(f"wo{hl}", [P, R, HID], F32R, attn) for hl in ("hi", "lo")}
            rawk = sb("rawk", [P, KT, P], F32, attn)
            rawv = sb("rawv", [P, KT, P], F32, attn)
            rawq = sb("rawq", [P, KT, R * P], F32, attn)
            rawo = sb("rawo", [P, R, HID], F32, attn)
            qkhi = sb("qkhi", [P, 2, ROPES, S], F32R, attn)
            qklo = sb("qklo", [P, 2, ROPES, S], F32R, attn)
            vt = sb("vt", [P, S], F32, attn)
            vhi = sb("vhi", [P, 2, NT, P], F32R, attn)
            vlo = sb("vlo", [P, 2, NT, P], F32R, attn)
            prob = [sb("prob0", [P, R, 3 * P], F32, attn), sb("prob1", [P, R, 4 * P], F32, attn)]
            pthi = sb("pthi", [P, NT, R * P], F32R, attn)
            ptlo = sb("ptlo", [P, NT, R * P], F32R, attn)
            ctxhi = sb("ctxhi", [P, R * P], F32R, attn)
            ctxlo = sb("ctxlo", [P, R * P], F32R, attn)
            ropeA = sb("ropeA", [P, 2, S], F32, attn)
            ropeB = sb("ropeB", [P, 2, S], F32, attn)
            ht = prob[0][:, :, :].rearrange("p a n -> p (a n)").rearrange("p (a n) -> p a n", n=S)
            HT = 3

            def flat(buf):
                return buf.rearrange("p a n -> p (a n)")

            wmt = {2: rawq, 3: rawo, 4: rawq, 5: rawo}
            baser = rawq
            base = {"hi": hThi[:, :, 0:HID], "lo": hTlo[:, :, 0:HID]}
            lar = rawo[:, 0, :].rearrange("p (t n) -> p t n", t=KT)
            la = {"hi": hThi[:, :, S:S + LORA_PAD], "lo": hTlo[:, :, S:S + LORA_PAD]}
            lbr = rawo[:, 1, :]
            lb = {hl: flat(wqkv[hl][:, V_, :, :]) for hl in ("hi", "lo")}
            xs = [rawo[:, 2, :], rawo[:, 3, :], rawq[:, 2, :], rawq[:, 3, :],
                  rawo[:, 0, :], rawo[:, 1, :], rawo[:, 2, :], rawo[:, 3, :]]
            bb = rawq[:, 0, :]
            ga_rows = [flat(rawk[:, :, :]), flat(rawv[:, :, :])]
            gb_rows = [ropeA[:, 0, :], ropeA[:, 1, :]]
            gbb = [cos, sin]
            ncol = vt[:, :].rearrange("p (f n) -> p f n", f=KT)
            ring = [ropeB[:, 0, :], ropeB[:, 1, :], vt[:, :], rawq[:, 0, :]]
            RING = len(ring)

            def h2(m):
                return ring[m % RING].rearrange("p (f n) -> p f n", f=KT)

            def h2s(hl, m):
                return wqkv[hl][:, (K_, QS[0], QS[2], QS[3])[m % RING], :, :]

            def lw(m):
                return rawq[:, 1, (m % 2) * P:(m % 2 + 1) * P]

            def lws(hl, m):
                return wqkv[hl][:, QS[1], m % 2, :]

            xT_bank = [ctx_bank] * (NT + 1) + [PS[0], PS[1], PS[2]]
            low_bank = [A_] * NT + [PS[3], PS[4]] * 2
            y_bank = [A_] * NT + [B_, A_] * 2
            bc_bank, mod_bank = PS[1], PS[2]
            MODC = 2 * KT * B

            def raw_item(k):
                if k == K_:
                    return rawk[:, :, :]
                if k == V_:
                    return rawv[:, :, :]
                return rawq[:, :, QS.index(k) * P:(QS.index(k) + 1) * P]

            def wait_raw(eng, g, k):
                eng.wait_ge(s_rawk if k == K_ else s_rawv if k == V_ else s_rawq, 16 * g + 16)

            def slot(g, b, i):
                return g * SLOTS + (NT * b + i)

            def unit(g, b):
                return g * B + b

            def pts(g, b, i):
                return g * (2 * TRI[NT]) + (b * TRI[NT] + TRI[i])

            def following(g, b, i):
                i += 1
                if i == NT:
                    i, b = 0, b + 1
                if b == B:
                    b, g = 0, g + 1
                return g, b, i

            def ahead(g, b, i, last):
                if last and b == 1:
                    return [], B_
                if i == NT - 1:
                    return ([] if last else [(g + 1, b, K_, A_), (g + 1, b, QS[0], B_)]), A_
                gn, bn = (g, 1) if b == 0 else (g + 1, 0)
                return {0: ([(gn, bn, V_, B_)], A_),
                        1: ([(gn, bn, QS[1], B_)], A_),
                        2: ([(gn, bn, QS[2], B_), (gn, bn, QS[3], A_)], B_)}[i]

            def late(g, b, i, last):
                if i == 0 and not (last and b == 1):
                    return ((g, 1) if b == 0 else (g + 1, 0)) + (QS[0],)
                if i == 3 and not (last and b == 1):
                    return ((g, 1) if b == 0 else (g + 1, 0)) + (QS[3],)
                return None

            def last_group(g):
                return isinstance(g, int) and g == G - 1

            def bc_before(b, i):
                return min(max(NT * b + i - 1, 0), 2 * B)

            def mods_before(b, i):
                return max(0, min(NT * b + i, len(VECTORS)))

            def rope_no(k):
                return 0 if k == K_ else 1 + QS.index(k)

            def parity(b, r):
                return (b * ROPES + r) % 2

            main = attn.enter_context(nc.Block())

            @main.sync
            def _(sp):
                xv = x.rearrange("b (t p) n -> b p t n", p=P)
                sp.dma_start(cT[:, :, :], c.rearrange("b (p t) -> p b t", t=KT)).then_inc(s_c, 16)
                wms = wmod.rearrange("(p t) n -> p t n", t=KT)
                sp.dma_start(rawo[:, :, :], wms[:, :, 0:HID]).then_inc(s_wm[0], 16)
                for h, half_ in enumerate((ropeA, ropeB)):
                    sp.dma_start(half_[:, :, :], wms[:, 2 * h:2 * h + 2, HID:2 * HID]).then_inc(s_wm[1], 16)
                sp.dma_start(acc[:, 0:NT, :], xv[0]).then_inc(s_x[0], 16)
                sp.dma_start(const[:, 3 * S:], consts[:, 3 * S:]).then_inc(s_ident, 16)
                sp.dma_start(bq_sb[:, :], bq).then_inc(s_bias, 16)
                sp.dma_start(bk_sb[:, :], bk).then_inc(s_bias, 16)
                sp.dma_start(bv_sb[:, :], bv).then_inc(s_bias, 16)
                sp.dma_start(rawk[:, :, :], Wk[0]).then_inc(s_rawk, 16)
                sp.dma_start(rawq[:, :, :], Wq[0]).then_inc(s_rawq, 16)
                sp.dma_start(rawv[:, :, :], Wv[0]).then_inc(s_rawv, 16)
                sp.dma_start(acc[:, NT:2 * NT, :], xv[1]).then_inc(s_x[1], 16)
                sp.dma_start(const[:, 0:3 * S], consts[:, 0:3 * S]).then_inc(s_const, 16)
                sp.wait_ge(s_modp, 1)
                sp.dma_start(rawo[:, :, :], Wo[0]).then_inc(s_rawo, 16)
                sp.wait_ge(s_xnT, B * KT)
                for t in range(B * NT):
                    sp.dma_start(acc[:, t, :], bo.broadcast_to([P, HID])).then_inc(s_bo, 16)

                def loads(g):
                    sp.wait_ge(s_wlo, g * ITEMS + ITEMS)
                    sp.dma_start(rawk[:, :, :], Wk[bass.ds(g + 1, 1)]).then_inc(s_rawk, 16)
                    sp.dma_start(rawv[:, :, :], Wv[bass.ds(g + 1, 1)]).then_inc(s_rawv, 16)
                    sp.dma_start(rawq[:, :, :], Wq[bass.ds(g + 1, 1)]).then_inc(s_rawq, 16)
                    sp.wait_ge(s_wolo, g * (R - 1) + (R - 1))
                    sp.wait_ge(s_wolo_pool, g + 1)
                    sp.dma_start(rawo[:, :, :], Wo[bass.ds(g + 1, 1)]).then_inc(s_rawo, 16)

                with sp.Fori(0, G - 1) as g:
                    loads(g)
                sp.wait_ge(s_bo, 16 * B * NT)
                xt = x.rearrange("b (t p) n -> (b t) p n", p=P)
                ot = out.rearrange("b (t p) n -> (b t) p n", p=P)

                def wm_load(v):
                    sp.dma_start(wmt[v][:, :, :], wms[:, :, v * HID:(v + 1) * HID]).then_inc(t_wm[v - 2], 16)

                def x_load(m):
                    sp.dma_start(xs[m], xt[m]).then_inc(t_x[m], 16)

                sp.wait_ge(s_wlo, G * ITEMS)
                wm_load(2)
                sp.dma_start(gw[:, :, :], gateT.rearrange("(t p) n -> p t n", p=P)).then_inc(t_gw, 16)
                sp.dma_start(io8[:, :], iota8.broadcast_to([P, E])).then_inc(t_gw, 16)
                sp.wait_ge(s_wolo, G * (R - 1))
                sp.wait_ge(s_wolo_pool, G)
                wm_load(3)
                sp.wait_ge(t_modp, 1)
                wm_load(4)
                sp.wait_ge(t_modp, 2)
                wm_load(5)
                sp.wait_ge(t_modp, 3)
                x_load(0)
                sp.dma_start(lar, loraAT.rearrange("(t p) n -> p t n", p=P)).then_inc(t_la, 16)
                sp.dma_start(baser[:, :, :], baseT.rearrange("(t p) n -> p t n", p=P)).then_inc(t_base, 16)
                x_load(1)
                sp.dma_start(lbr, loraB).then_inc(t_lb, 16)
                sp.wait_ge(t_baselo, KT)
                x_load(2)
                sp.dma_start(bb, base_b.broadcast_to([P, HID])).then_inc(t_bb, 16)
                x_load(3)
                sp.wait_ge(t_lalo, 1)
                x_load(4)
                sp.wait_ge(t_lblo, 1)
                x_load(5)
                for m in (6, 7):
                    sp.wait_ge(t_xT, m - 5)
                    x_load(m)
                for m in range(NM):
                    if m < NM - 1:
                        sp.wait_ge(t_out, m + 1)
                    else:
                        sp.wait_ge(t_outlast, 1)
                    sp.dma_start(ot[m], acc[:, m, :]).then_inc(t_done, 16)
                sp.wait_ge(t_done, 16 * NM)

            @main.tensor
            def _(pe):
                def three(out, whi, wlo, xhi, xlo, start, stop):
                    nc.tensor.matmul(out, whi, xhi, start=start, stop=False)
                    nc.tensor.matmul(out, whi, xlo, start=False, stop=False)
                    return nc.tensor.matmul(out, wlo, xhi, start=False, stop=stop)

                def project(g, b, k, bank, tiles=range(KT)):
                    if tiles[0] == 0:
                        pe.wait_ge(s_wlo, g * ITEMS + (k + 1))
                    for t in tiles:
                        last = three(bank[:, :], wqkv["hi"][:, k, t, :], wqkv["lo"][:, k, t, :],
                                     hThi[:, t, b * S:(b + 1) * S], hTlo[:, t, b * S:(b + 1) * S],
                                     t == 0, t == KT - 1)
                    if tiles[-1] == KT - 1:
                        last.then_inc(s_proj, 1)

                def turn_v(g, b):
                    pe.wait_ge(s_vt, unit(g, b) + 1)
                    for t in range(NT):
                        last = nc.tensor.transpose(pt_bank[1][:, t * P:(t + 1) * P], vt[:, t * P:(t + 1) * P], ident)
                    last.then_inc(s_vtr, 1)

                def scores(g, b, i, h, first=False):
                    n = slot(g, b, i)
                    if i == 0:
                        pe.wait_ge(s_qklo, unit(g, b) * ROPES + (h + 2))
                    if last_group(g) and h == 1 and bc_before(b, i - 1):
                        pe.wait_ge(t_bcd, bc_before(b, i - 1))
                    if last_group(g) and h == 2 and mods_before(b, i - 1):
                        pe.wait_ge(t_mod, mods_before(b, i - 1))
                    if not first or h == 3:
                        pe.wait_ge(s_exp, {0: n * R, 1: n * R - 2, 2: n * R - 1, 3: n * R + 1}[h])
                    w = max(2, i + 1) * P
                    q = slice(i * P, (i + 1) * P)
                    three(s_bank[h][:, 0:w], qkhi[:, b, 1 + h, q], qklo[:, b, 1 + h, q],
                          qkhi[:, b, 0, 0:w], qklo[:, b, 0, 0:w], True, True).then_inc(s_scores, 1)

                def turn(g, b, i, j):
                    if j == 0:
                        pe.wait_ge(s_prob, slot(g, b, i) * R + R)
                    if j == 1 and i == 1 and vt_ahead:
                        pe.wait_ge(s_vlo, unit(g, b) + 2)
                    if j >= 2:
                        pe.wait_ge(s_ptlo, pts(g, b, i) + (j - 1))
                    for h in range(R):
                        last = nc.tensor.transpose(pt_bank[j % 2][:, h * P:(h + 1) * P],
                                                   prob[i % 2][:, h, j * P:(j + 1) * P], ident)
                    last.then_inc(s_pt, 1)

                def values(g, b, i, tiles):
                    if last_group(g) and b == 1 and tiles[0] == 0:
                        pe.wait_ge(t_h, KT * (i + 1))
                    for j in tiles:
                        pe.wait_ge(s_ptlo, pts(g, b, i) + (j + 1))
                        last = three(ctx_bank[:, :], vhi[:, b, j, :], vlo[:, b, j, :],
                                     pthi[:, j, :], ptlo[:, j, :], j == 0, j == i)
                    if tiles[-1] == i:
                        last.then_inc(s_ctx, 1)

                def output(g, b, i, bank):
                    pe.wait_ge(s_ctxlo, slot(g, b, i) + 1)
                    for h in range(R):
                        if (b, i) == (0, 0):
                            if h == WO_ORDER[WO_POOL]:
                                pe.wait_ge(s_wolo_pool, g + 1)
                            else:
                                k = WO_ORDER.index(h)
                                pe.wait_ge(s_wolo, g * (R - 1) + (k + 1 if k < WO_POOL else k))
                        last = three(bank[:, :], ctxhi[:, h * P:(h + 1) * P], ctxlo[:, h * P:(h + 1) * P],
                                     wo["hi"][:, h, :], wo["lo"][:, h, :], h == 0, h == R - 1)
                    last.then_inc(s_o, 1)

                def bank_free(g, b, i, what):
                    n, ropes = slot(g, b, i), (unit(g, b) + 1) * ROPES
                    if what == "out":
                        if i <= 1 or (b == 1 and not items):
                            pe.wait_ge(s_acc, n + 1)
                        elif i == 2:
                            pe.wait_ge(s_rope, ropes + 4)
                        else:
                            pe.wait_ge(s_rope, ropes + (ROPES + 1 if items else ROPES))
                    elif what == V_:
                        pe.wait_ge(s_rope, ropes + 2)
                    elif what == QS[1]:
                        pe.wait_ge(s_vt, unit(g, b) + 2)
                    elif what == QS[2]:
                        pe.wait_ge(s_rope, ropes + 3)
                    elif what == K_:
                        pe.wait_ge(s_rope, ropes + 5)
                    else:
                        pe.wait_ge(s_acc, n + 1)

                pe.wait_ge(s_silu, 1)
                modp = PS[5]
                for v, src in ((0, lambda t: rawo[:, t, :]), (1, lambda t: (ropeA, ropeB)[t // 2][:, t % 2, :])):
                    pe.wait_ge(s_wm[v], 16 if v == 0 else 32)
                    for f in range(KT):
                        for t in range(KT):
                            last = nc.tensor.matmul(modp[:, (v * KT + f) * B:(v * KT + f + 1) * B],
                                                    src(t)[:, f * P:(f + 1) * P], siluT[:, t, :],
                                                    start=t == 0, stop=t == KT - 1)
                last.then_inc(s_modp, 1)
                pe.wait_ge(s_ident, 16)

                def turn_x(b):
                    for f in range(KT):
                        m = b * KT + f
                        if f == 0:
                            pe.wait_ge(s_xn, (b + 1) * NT)
                        if m >= 4:
                            pe.wait_ge(s_ht, m - 3)
                        for t in range(NT):
                            src = (prob[1] if b == 0 else acc)[:, b * NT + t, f * P:(f + 1) * P]
                            last = nc.tensor.transpose(PS[m % 4][:, t * P:(t + 1) * P], src, ident)
                        last.then_inc(s_xnT, 1)

                turn_x(0)
                pe.wait_ge(s_hlo, KT)
                project(0, 0, K_, A_)
                project(0, 0, QS[0], B_)
                pe.wait_ge(s_rope, 1)
                project(0, 0, V_, A_)
                pe.wait_ge(s_rope, 2)
                project(0, 0, QS[1], B_)
                turn_x(1)
                pe.wait_ge(s_vt, 1)
                project(0, 0, QS[2], A_)
                pe.wait_ge(s_rope, 3)
                project(0, 0, QS[3], B_)
                turn_v(0, 0)
                pe.wait_ge(s_hlo, 2 * KT)
                pe.wait_ge(s_rope, 4)
                project(0, 1, K_, A_)
                for h in range(R):
                    scores(0, 0, 0, h, first=True)
                pe.wait_ge(s_rope, 5)
                project(0, 1, QS[0], B_)

                def vectors(b, i):
                    pe.wait_ge(s_exp, (slot(G - 1, b, i) + 1) * R + 3)
                    for q, v in enumerate(VECTORS[i]):
                        pe.wait_ge(t_wm[v - 2], 16)
                        for f in range(KT):
                            for t in range(KT):
                                last = nc.tensor.matmul(mod_bank[:, (q * KT + f) * B:(q * KT + f + 1) * B],
                                                        wmt[v][:, t, f * P:(f + 1) * P], siluT[:, t, :],
                                                        start=t == 0, stop=t == KT - 1)
                    last.then_inc(t_modp, 1)

                def broadcast(b, i):
                    pe.wait_ge(s_exp, (slot(G - 1, b, i) + 1) * R + 2)
                    pe.wait_ge(t_ncol, bc_before(b, i) + 1)
                    for f in range(KT):
                        last = nc.tensor.matmul(bc_bank[:, f * P:(f + 1) * P], ncol[:, f, :], ident,
                                                start=True, stop=True)
                    last.then_inc(t_bc, 1)

                def turn_rows(m):
                    pe.wait_ge(t_xn, m + 1)
                    for f in range(KT):
                        last = nc.tensor.transpose(xT_bank[m][:, f * P:(f + 1) * P],
                                                   xs[m][:, f * P:(f + 1) * P], ident)
                    last.then_inc(t_xT, 1)

                def low_rank(m):
                    if m == 0:
                        pe.wait_ge(t_gw, 32)
                        pe.wait_ge(s_acc, slot(G - 1, 1, 0) + 1)
                    elif m < NT:
                        pe.wait_ge(t_prod, m)
                    elif m >= NT + 2:
                        pe.wait_ge(t_lwlo, m - 1)
                    pe.wait_ge(t_h, KT * (m + 1))
                    bank = low_bank[m]
                    for t in range(KT):
                        last = nc.tensor.matmul(bank[:, LORA_PAD:LORA_PAD + E], h2(m)[:, t, :], gw[:, t, :],
                                                start=t == 0, stop=t == KT - 1)
                    last.then_inc(t_gate, 1)
                    if m == 0:
                        pe.wait_ge(t_lalo, 1)
                    pe.wait_ge(t_hlo, m + 1)
                    for t in range(KT):
                        last = three(bank[:, 0:LORA_PAD], h2s("hi", m)[:, t, :], h2s("lo", m)[:, t, :],
                                     la["hi"][:, t, :], la["lo"][:, t, :], t == 0, t == KT - 1)
                    last.then_inc(t_low, 1)

                def turn_low(m):
                    pe.wait_ge(t_lw, m + 1)
                    nc.tensor.transpose(low_bank[m][:, 3 * P:4 * P], lw(m), ident).then_inc(t_lwT, 1)

                def linear(m):
                    if m == 0:
                        pe.wait_ge(t_baselo, KT)
                    if m < NT:
                        pe.wait_ge(t_lwlo, m + 1)
                    elif m > NT:
                        pe.wait_ge(t_prod, m - 1)
                    else:
                        pe.wait_ge(s_acc, G * SLOTS + 1)
                    for t in range(KT):
                        three(y_bank[m][:, :], h2s("hi", m)[:, t, :], h2s("lo", m)[:, t, :],
                              base["hi"][:, t, :], base["lo"][:, t, :], t == 0, False)

                def experts(m):
                    if m == 0:
                        pe.wait_ge(t_lblo, 1)
                    pe.wait_ge(t_lwlo, m + 1)
                    three(y_bank[m][:, :], lws("hi", m), lws("lo", m), lb["hi"], lb["lo"], False, True)\
                        .then_inc(t_y, 1)

                def slots(g, b, i, last):
                    nonlocal items, vt_ahead
                    second = last and b == 1
                    items, obank = ahead(g, b, i, last)
                    vt_ahead = not (last and b == 1)
                    nxt = following(g, b, i)
                    more = not (last and (b, i) == (B - 1, NT - 1))
                    parts = [(item, t) for item in items for t in range(KT)]

                    def fill(n):
                        for item, t in parts[:n]:
                            if t == 0:
                                bank_free(g, b, i, item[2])
                            project(*item, range(t, t + 1))
                        del parts[:n]

                    def fill_rows(step, m):
                        if second and m >= 0:
                            step(m)

                    def score(h):
                        if more:
                            scores(*nxt, h)

                    score(0)
                    turn(g, b, i, 0)
                    score(1)
                    if i >= 1:
                        turn(g, b, i, 1)
                    score(2)
                    fill(FILLS[i][0])
                    if i == 3:
                        turn(g, b, i, 2)
                    score(3)
                    if i == 2:
                        turn(g, b, i, 2)
                    fill(FILLS[i][1])
                    if i == 3:
                        turn(g, b, i, 3)
                        fill(FILLS[i][2])
                    fill_rows(turn_low, i - 1)
                    values(g, b, i, range(0, min(i + 1, 2)))
                    fill_rows(linear, i - 1)
                    fill_rows(experts, i - 1)
                    if i >= 2:
                        fill(FILLS[i][-2])
                        values(g, b, i, range(2, i + 1))
                    fill(FILLS[i][-1])
                    fill_rows(low_rank, i)
                    bank_free(g, b, i, "out")
                    output(g, b, i, obank)
                    if items and items[0][2] == V_:
                        turn_v(items[0][0], items[0][1])
                    if last and b == 0 and i in VECTORS:
                        vectors(b, i)
                    if last and bc_before(*following(g, b, i)[1:]) > bc_before(b, i) and more:
                        broadcast(b, i)
                    if last and (b == 1 or i == NT - 1):
                        turn_rows(0 if b == 0 else i + 1)

                items, vt_ahead = [], True
                with pe.Fori(0, G - 1) as g:
                    for b in range(B):
                        for i in range(NT):
                            slots(g, b, i, False)
                for b in range(B):
                    for i in range(NT):
                        slots(G - 1, b, i, True)
                turn_low(NT - 1)
                turn_rows(NT + 1)
                linear(NT - 1)
                experts(NT - 1)
                low_rank(NT)
                turn_rows(NT + 2)
                for m in range(NT, NM):
                    if m + 1 < NM:
                        low_rank(m + 1)
                    if m > NT:
                        experts(m - 1)
                    linear(m)
                    if m == NT:
                        turn_rows(NT + 3)
                    turn_low(m)
                experts(NM - 1)

            @main.scalar
            def _(act):
                def whi(g, k):
                    wait_raw(act, g, k)
                    nc.scalar.activation(wqkv["hi"][:, k, :, :], raw_item(k), ACT.Copy).then_inc(s_whi, 1)

                def qk_high(g, b, k):
                    r = rope_no(k)
                    act.wait_ge(s_rot, unit(g, b) * ROPES + (r + 1))
                    nc.scalar.activation(qkhi[:, b, r, :], ropeA[:, parity(b, r), :], ACT.Copy).then_inc(s_qkhi, 1)

                def v_copy(g, b):
                    act.wait_ge(s_proj, unit(g, b) * ITEMS + (V_ + 1))
                    nc.scalar.activation(vt[:, :], A_[:, :] if prologue else B_[:, :], ACT.Identity,
                                         bias=bv_sb[:, bass.ds(g, 1)]).then_inc(s_vt, 1)

                def v_high(g, b):
                    act.wait_ge(s_vtr, unit(g, b) + 1)
                    nc.scalar.activation(vhi[:, b, :, :], pt_bank[1][:, :].rearrange("p (t d) -> p t d", t=NT),
                                         ACT.Copy).then_inc(s_vhi, 1)

                def exponent(g, b, i, h):
                    act.wait_ge(s_negmax, slot(g, b, i) * R + (h + 1))
                    nc.scalar.activation(prob[i % 2][:, h, 0:(i + 1) * P], s_bank[h][:, 0:(i + 1) * P], ACT.Exp,
                                         bias=negmax[:, i % 2, h:h + 1], scale=-1.0,
                                         accum_out=rowsum[:, i % 2, h:h + 1]).then_inc(s_exp, 1)

                def pt_high(g, b, i, j):
                    act.wait_ge(s_pt, pts(g, b, i) + (j + 1))
                    nc.scalar.activation(pthi[:, j, :], pt_bank[j % 2][:, :], ACT.Copy).then_inc(s_pthi, 1)

                def base_high(t):
                    act.wait_ge(t_base, 16)
                    nc.scalar.activation(base["hi"][:, t, :], baser[:, t, :], ACT.Copy).then_inc(t_basehi, 1)

                def modulate_rows(m):
                    act.wait_ge(t_xT, m + 1)
                    if m == 0:
                        act.wait_ge(s_qklo, G * B * ROPES)
                        act.wait_ge(t_mod, len(VECTORS))
                    elif m == 2:
                        act.wait_ge(t_bc, 2 * B)
                    elif m == 3:
                        act.wait_ge(t_gbb, 1)
                    elif m >= RING:
                        act.wait_ge(t_out, m - RING + 1)
                    b = m // NT
                    for f in range(KT):
                        nc.scalar.activation(h2(m)[:, f, :], xT_bank[m][:, f * P:(f + 1) * P], ACT.Identity,
                                             bias=modT[:, 3, f, b:b + 1], scale=modT[:, 4, f, b:b + 1])\
                            .then_inc(t_h, 1)
                    act.wait_ge(t_h, KT * (m + 1))
                    if m >= RING:
                        act.wait_ge(t_y, m - RING + 1)
                    nc.scalar.activation(h2s("hi", m), h2(m), ACT.Copy).then_inc(t_hhi, 1)

                def gate_exp(m):
                    act.wait_ge(t_diff, m + 1)
                    nc.scalar.activation(small[:, 1:2], small[:, 0:1], ACT.Exp).then_inc(t_e, 1)

                def low_high(m):
                    act.wait_ge(t_lwT, m + 1)
                    nc.scalar.activation(lws("hi", m), low_bank[m][:, 3 * P:4 * P], ACT.Copy).then_inc(t_lwhi, 1)

                act.wait_ge(s_c, 16)
                nc.scalar.activation(siluT[:, :, :], cT[:, :, :].rearrange("p b t -> p t b"), ACT.Exp, scale=-1.0)\
                    .then_inc(s_expc, 1)
                for k in range(ITEMS):
                    whi(0, k)
                act.wait_ge(s_bias, 48)
                prologue = True

                def modulate(b):
                    act.wait_ge(s_mod, 1)
                    for m in range(b * KT, (b + 1) * KT):
                        if m >= HT:
                            act.wait_ge(s_hlo, m - HT + 1)
                        act.wait_ge(s_xnT, m + 1)
                        nc.scalar.activation(ht[:, m % HT, :], PS[m % 4][:, :], ACT.Identity,
                                             bias=modT[:, 0, m % KT, b:b + 1], scale=modT[:, 1, m % KT, b:b + 1])\
                            .then_inc(s_ht, 1)

                modulate(0)
                qk_high(0, 0, K_)
                qk_high(0, 0, QS[0])
                v_copy(0, 0)
                modulate(1)
                for k in QS[1:]:
                    qk_high(0, 0, k)
                v_high(0, 0)
                qk_high(0, 1, K_)
                prologue = False
                for h in range(R):
                    exponent(0, 0, 0, h)

                def slots(g, b, i, last):
                    items, _ = ahead(g, b, i, last)
                    nxt = following(g, b, i)
                    more = not (last and (b, i) == (B - 1, NT - 1))
                    left = late(g, b, i, last)
                    second = last and b == 1

                    def exp(h):
                        if more:
                            exponent(*nxt, h)

                    def ctx_high():
                        act.wait_ge(s_ctx, slot(g, b, i) + 1)
                        nc.scalar.activation(ctxhi[:, :], ctx_bank[:, :], ACT.Copy).then_inc(s_ctxhi, 1)

                    def wo_high(h):
                        if (b, i) == (0, 0):
                            if h == WO_ORDER[0]:
                                act.wait_ge(s_rawo, 16 * g + 16)
                                act.wait_ge(s_acc, g * SLOTS + 1)
                            nc.scalar.activation(wo["hi"][:, h, :], rawo[:, h, :], ACT.Copy).then_inc(s_wohi, 1)

                    if left:
                        qk_high(*left)
                    exp(0)
                    pt_high(g, b, i, 0)
                    exp(1)
                    wo_high(WO_ORDER[0])
                    wo_high(WO_ORDER[1])
                    if i >= 1:
                        pt_high(g, b, i, 1)
                    if second:
                        modulate_rows(i)
                    exp(2)
                    if (b, i) == (0, 0):
                        ctx_high()
                        wo_high(WO_ORDER[2])
                    if i == 3:
                        pt_high(g, b, i, 2)
                    exp(3)
                    if i >= 2:
                        pt_high(g, b, i, i)
                    wo_high(WO_ORDER[3])
                    if second and i >= 1:
                        low_high(i - 1)
                    def next_weights():
                        for k in ([] if last else SPLIT_AT.get((b, i), [])):
                            act.wait_ge(s_proj, g * (2 * ITEMS) + (ITEMS + k + 1))
                            whi(g + 1, k)

                    if i == 3:
                        next_weights()
                    if (b, i) != (0, 0):
                        ctx_high()
                    if second:
                        gate_exp(i)
                    if last and (b, i) == (0, 3):
                        act.wait_ge(s_proj, G * B * ITEMS)
                        act.wait_ge(t_la, 16)
                        nc.scalar.activation(la["hi"][:, :, 0:P], lar, ACT.Copy).then_inc(t_lahi, 1)
                        base_high(0)
                        base_high(1)
                    if last and (b, i) == (1, 0):
                        base_high(2)
                        base_high(3)
                        act.wait_ge(t_lb, 16)
                        nc.scalar.activation(lb["hi"], lbr, ACT.Copy).then_inc(t_lbhi, 1)
                    if items and items[0][2] == V_:
                        v_copy(items[0][0], items[0][1])
                        next_weights()
                        v_high(items[0][0], items[0][1])
                    elif items:
                        qk_high(*items[0][:3])

                with act.Fori(0, G - 1) as g:
                    for b in range(B):
                        for i in range(NT):
                            slots(g, b, i, False)
                for b in range(B):
                    for i in range(NT):
                        slots(G - 1, b, i, True)
                modulate_rows(NT)
                low_high(NT - 1)
                modulate_rows(NT + 1)
                for m in range(NT, NM):
                    gate_exp(m)
                    if m + 2 < NM:
                        modulate_rows(m + 2)
                    low_high(m)

            @main.gpsimd
            def _(pool):
                def wlow(g, k):
                    pool.wait_ge(s_whi, g * ITEMS + (k + 1))
                    nc.gpsimd.tensor_tensor(wqkv["lo"][:, k, :, :], raw_item(k),
                                            wqkv["hi"][:, k, :, :].bitcast(F32), ALU.subtract).then_inc(s_wlo, 1)

                def rotate(g, b, k):
                    r = rope_no(k)
                    q = parity(b, r)
                    pool.wait_ge(s_rope, unit(g, b) * ROPES + (r + 1))
                    nc.gpsimd.tensor_tensor(ropeA[:, q, :], ropeA[:, q, :], ropeB[:, q, :], ALU.add).then_inc(s_rot, 1)

                def qk_low(g, b, k):
                    r = rope_no(k)
                    pool.wait_ge(s_qkhi, unit(g, b) * ROPES + (r + 1))
                    nc.gpsimd.tensor_tensor(qklo[:, b, r, :], ropeA[:, parity(b, r), :],
                                            qkhi[:, b, r, :].bitcast(F32), ALU.subtract).then_inc(s_qklo, 1)

                def normalise(g, b, i, h):
                    if h % 2 == 0:
                        pool.wait_ge(s_rinv, slot(g, b, i) * 2 + (h // 2 + 1))
                    p = prob[i % 2][:, h, 0:(i + 1) * P]
                    nc.gpsimd.tensor_tensor(p, p, rinv[:, i % 2, h:h + 1].to_broadcast([P, (i + 1) * P]),
                                            ALU.mult).then_inc(s_prob, 1)

                def deviation(b):
                    pool.wait_ge(s_var, b + 1)
                    cols = slice(b * NT, (b + 1) * NT)
                    nc.gpsimd.tensor_tensor(rstd[:, cols], var[:, cols], half[:, cols], ALU.pow).then_inc(s_rstd, 1)

                chain = [0]

                def link(ins):
                    chain[0] += 1
                    ins.then_inc(t_pool, 1)
                    pool.wait_ge(t_pool, chain[0])

                def gated(m):
                    a = acc[:, m, :]
                    pool.wait_ge(s_acc, slot(G - 1, m // NT, m % NT) + 2)
                    pool.wait_ge(t_bcd, m // NT + 1)
                    link(nc.gpsimd.tensor_tensor(a, a, ga_rows[m // NT], ALU.mult))
                    pool.wait_ge(t_x[m], 16)
                    nc.gpsimd.tensor_tensor(a, a, xs[m], ALU.add).then_inc(t_gated, 1)

                def deviation_rows(m):
                    pool.wait_ge(t_var, m + 1)
                    nc.gpsimd.tensor_tensor(rstd[:, m:m + 1], var[:, m:m + 1], half[:, m:m + 1], ALU.pow)\
                        .then_inc(t_rstd, 1)

                def add_bias(m):
                    pool.wait_ge(t_gbb, m // NT + 1)
                    pool.wait_ge(t_xn, m + 1)
                    link(nc.gpsimd.tensor_tensor(acc[:, m, :], acc[:, m, :], gbb[m // NT], ALU.add))

                def finish(m):
                    pool.wait_ge(t_prod, m + 1)
                    nc.gpsimd.tensor_tensor(acc[:, m, :], acc[:, m, :], ring[m % RING], ALU.add).then_inc(t_out, 1)

                nc.gpsimd.memset(half[:, :], -0.5).then_inc(s_half, 1)
                pool.wait_ge(s_half, 1)
                deviation(0)
                deviation(1)
                for k in [K_] + QS:
                    rotate(0, 0, k)
                    qk_low(0, 0, k)
                rotate(0, 1, K_)
                qk_low(0, 1, K_)
                for h in range(R):
                    normalise(0, 0, 0, h)
                rotate(0, 1, QS[0])

                def slots(g, b, i, last):
                    items, _ = ahead(g, b, i, last)
                    nxt = following(g, b, i)
                    more = not (last and (b, i) == (B - 1, NT - 1))
                    left = late(g, b, i, last)
                    if left:
                        qk_low(*left)
                    for h in range(R):
                        if more:
                            normalise(*nxt, h)
                        if h == 1 and (b, i) == (0, 0):
                            w = WO_ORDER[WO_POOL]
                            pool.wait_ge(s_wohi, g * R + (WO_POOL + 1))
                            nc.gpsimd.tensor_tensor(wo["lo"][:, w, :], rawo[:, w, :], wo["hi"][:, w, :].bitcast(F32),
                                                    ALU.subtract).then_inc(s_wolo_pool, 1)
                    for k in ([] if last else SPLIT_AT.get((b, i), [])):
                        wlow(g + 1, k)
                    if items and items[0][2] != V_:
                        rotate(*items[0][:3])
                        qk_low(*items[0][:3])
                    if len(items) > 1:
                        rotate(*items[1][:3])
                    if last and (b, i) == (0, 3):
                        gated(0)
                        pool.wait_ge(t_lahi, 1)
                        nc.gpsimd.tensor_tensor(la["lo"][:, :, 0:P], lar, la["hi"][:, :, 0:P].bitcast(F32),
                                                ALU.subtract).then_inc(t_lalo, 1)
                        deviation_rows(0)
                        gated(1)
                    if last and b == 1:
                        deviation_rows(i + 1)
                        if i == 0:
                            pool.wait_ge(t_lbhi, 1)
                            nc.gpsimd.tensor_tensor(lb["lo"], lbr, lb["hi"].bitcast(F32), ALU.subtract)\
                                .then_inc(t_lblo, 1)
                        gated(i + 2)
                        if i >= 1:
                            add_bias(i - 1)
                            finish(i - 1)

                with pool.Fori(0, G - 1) as g:
                    for b in range(B):
                        for i in range(NT):
                            slots(g, b, i, False)
                for b in range(B):
                    for i in range(NT):
                        slots(G - 1, b, i, True)
                deviation_rows(NT + 1)
                gated(NT + 2)
                deviation_rows(NT + 2)
                add_bias(NT - 1)
                finish(NT - 1)
                gated(NT + 3)
                deviation_rows(NT + 3)
                for m in range(NT, NM):
                    add_bias(m)
                    if m < NM - 1:
                        finish(m)

            @main.vector
            def _(dve):
                chain = [0]

                def link(ins):
                    chain[0] += 1
                    ins.then_inc(s_dve, 1)
                    dve.wait_ge(s_dve, chain[0])

                def rope(g, b, k, bank):
                    r = rope_no(k)
                    q = parity(b, r)
                    item = unit(g, b) * ROPES + r
                    if not (isinstance(g, int) and g == 0 and b == 0 and r < 2):
                        dve.wait_ge(s_qklo, item - 1)
                    dve.wait_ge(s_proj, unit(g, b) * ITEMS + (k + 1))
                    if k == K_:
                        lo, hi = bk_sb[0:64, bass.ds(g, 1)], bk_sb[64:128, bass.ds(g, 1)]
                        both = bk_sb[:, bass.ds(g, 1)]
                    else:
                        at = bass.ds(g * R + QS.index(k), 1)
                        lo, hi, both = bq_sb[0:64, at], bq_sb[64:128, at], bq_sb[:, at]
                    nc.vector.scalar_tensor_tensor(out=ropeA[:, q, :], in0=bank[:, :], scalar=both, in1=cos,
                                                   op0=ALU.add, op1=ALU.mult)
                    nc.vector.scalar_tensor_tensor(out=ropeB[0:64, q, :], in0=bank[64:128, :], scalar=hi,
                                                   in1=sin[64:128, :], op0=ALU.add, op1=ALU.mult)
                    nc.vector.scalar_tensor_tensor(out=ropeB[64:128, q, :], in0=bank[0:64, :], scalar=lo,
                                                   in1=sin[0:64, :], op0=ALU.add, op1=ALU.mult).then_inc(s_rope, 1)

                def v_low(g, b):
                    dve.wait_ge(s_vhi, unit(g, b) + 1)
                    nc.vector.tensor_tensor(vlo[:, b, :, :], pt_bank[1][:, :].rearrange("p (t d) -> p t d", t=NT),
                                            vhi[:, b, :, :].bitcast(F32), ALU.subtract).then_inc(s_vlo, 1)

                def maximum(g, b, i, h):
                    w = (i + 1) * P
                    dve.wait_ge(s_scores, slot(g, b, i) * R + (h + 1))
                    dve.nop(nofuse=True)
                    nc.vector.tensor_tensor_reduce(out=s_bank[h][:, 0:w], in0=s_bank[h][:, 0:w], in1=mask[:, S - w:S],
                                                   scale=-SCALE, scalar=3.0e38, op0=ALU.add, op1=ALU.min,
                                                   accum_out=negmax[:, i % 2, h:h + 1]).then_inc(s_negmax, 1)

                def invert(g, b, i, pair):
                    dve.wait_ge(s_exp, slot(g, b, i) * R + (2 * pair + 2))
                    nc.vector.reciprocal(rinv[:, i % 2, 2 * pair:2 * pair + 2],
                                         rowsum[:, i % 2, 2 * pair:2 * pair + 2]).then_inc(s_rinv, 1)

                def pt_low(g, b, i, j):
                    dve.wait_ge(s_pthi, pts(g, b, i) + (j + 1))
                    nc.vector.tensor_tensor(ptlo[:, j, :], pt_bank[j % 2][:, :], pthi[:, j, :].bitcast(F32),
                                            ALU.subtract).then_inc(s_ptlo, 1)

                def copy_vectors(i):
                    dve.wait_ge(t_modp, i + 1)
                    vs = VECTORS[i]
                    copy = nc.vector.tensor_copy(modT[:, vs[0]:vs[-1] + 1, :, :].rearrange("p v f b -> p (v f b)"),
                                                 mod_bank[:, 0:len(vs) * KT * B])
                    if 4 in vs:
                        link(copy)
                        copy = nc.vector.tensor_scalar(modT[:, 4, :, :], modT[:, 4, :, :], 1.0, None, ALU.add)
                    copy.then_inc(t_mod, 1)
                    if vs[-1] in (2, 5):
                        dve.wait_ge(t_mod, i + 1)
                        m = modT[:, vs[-1], :, :].rearrange("p f b -> p (f b)")
                        s, n = neg[:, 0, :], neg[:, 1, :]
                        link(nc.vector.tensor_scalar(s, m, 0.0, 2.0, ALU.is_ge, ALU.mult))
                        link(nc.vector.tensor_scalar(s, s, -1.0, None, ALU.add))
                        link(nc.vector.tensor_tensor(n, s, m, ALU.mult))
                        link(nc.vector.tensor_scalar(n, n, 0.25, None, ALU.max))
                        link(nc.vector.tensor_tensor(m, s, n, ALU.mult))

                def repeat(k):
                    nc.vector.tensor_copy(ncol, modT[:, (2, 5)[k // B], :, k % B:k % B + 1].to_broadcast([P, KT, P]))\
                        .then_inc(t_ncol, 1)

                def copy_row(k):
                    dve.wait_ge(t_bc, k + 1)
                    nc.vector.tensor_copy((ga_rows + gb_rows)[k], bc_bank[:, :]).then_inc(t_bcd, 1)

                def bias_row(b):
                    dve.wait_ge(t_bb, 16)
                    nc.vector.tensor_tensor(gbb[b], bb, gb_rows[b], ALU.mult).then_inc(t_gbb, 1)

                def base_low(t):
                    dve.wait_ge(t_basehi, t + 1)
                    nc.vector.tensor_tensor(base["lo"][:, t, :], baser[:, t, :], base["hi"][:, t, :].bitcast(F32),
                                            ALU.subtract).then_inc(t_baselo, 1)

                def row_stats(m):
                    dve.wait_ge(t_gated, m + 1)
                    link(nc.vector.bn_stats(stats[:, m, :], acc[:, m, :]))
                    link(nc.vector.bn_aggr(mv[:, m, :], stats[:, m, :]))
                    nc.vector.tensor_scalar(var[:, m:m + 1], mv[:, m, 1:2], EPS, None, ALU.add).then_inc(t_var, 1)

                def norm_rows(m):
                    dve.wait_ge(t_rstd, m + 1)
                    nc.vector.tensor_scalar(xs[m], acc[:, m, :], mv[:, m, 0:1], rstd[:, m:m + 1],
                                            ALU.subtract, ALU.mult).then_inc(t_xn, 1)

                def rows_low(m):
                    dve.wait_ge(t_hhi, m + 1)
                    nc.vector.tensor_tensor(h2s("lo", m), h2(m), h2s("hi", m).bitcast(F32),
                                            ALU.subtract).then_inc(t_hlo, 1)

                def route(m):
                    dve.wait_ge(t_low, m + 1)
                    if m == 0:
                        dve.wait_ge(t_gw, 32)
                    link(nc.vector.tensor_copy(logit[:, :], low_bank[m][:, LORA_PAD:LORA_PAD + E]))
                    link(nc.vector.max(top[:, :], logit[:, :]))
                    link(nc.vector.max_index(topi[:, :], top[:, :], logit[:, :]))
                    link(nc.vector.tensor_copy(small[:, 4:6], topi[:, 0:2]))
                    nc.vector.tensor_tensor(small[:, 0:1], top[:, 1:2], top[:, 0:1], ALU.subtract).then_inc(t_diff, 1)

                def weigh(m):
                    dve.wait_ge(t_e, m + 1)
                    link(nc.vector.tensor_scalar(small[:, 2:3], small[:, 1:2], 1.0, 0.5, ALU.add, ALU.mult))
                    link(nc.vector.reciprocal(small[:, 2:3], small[:, 2:3]))
                    link(nc.vector.tensor_tensor(small[:, 3:4], small[:, 1:2], small[:, 2:3], ALU.mult))
                    for k in range(2):
                        last = nc.vector.tensor_scalar(oneh[:, k, :], io8[:, :], small[:, 4 + k:5 + k],
                                                       small[:, 2 + k:3 + k], ALU.is_equal, ALU.mult)
                    link(last)
                    link(nc.vector.tensor_tensor(oneh[:, 0, :], oneh[:, 0, :], oneh[:, 1, :], ALU.add))
                    if m >= 2:
                        dve.wait_ge(t_lwT, m - 1)
                    nc.vector.tensor_tensor(lw(m).rearrange("p (e r) -> p e r", e=E),
                                            low_bank[m][:, 0:P].rearrange("p (e r) -> p e r", e=E),
                                            oneh[:, 0, :].unsqueeze(2).to_broadcast([P, E, RANK]), ALU.mult)\
                        .then_inc(t_lw, 1)

                def low_low(m):
                    dve.wait_ge(t_lwhi, m + 1)
                    nc.vector.tensor_tensor(lws("lo", m), low_bank[m][:, 3 * P:4 * P], lws("hi", m).bitcast(F32),
                                            ALU.subtract).then_inc(t_lwlo, 1)

                def gate_product(m):
                    dve.wait_ge(t_y, m + 1)
                    nc.vector.tensor_tensor(ring[m % RING], y_bank[m][:, :], gb_rows[m // NT], ALU.mult)\
                        .then_inc(t_prod, 1)

                dve.wait_ge(s_expc, 1)
                link(nc.vector.tensor_scalar(siluT[:, :, :], siluT[:, :, :], 1.0, None, ALU.add))
                link(nc.vector.reciprocal(siluT[:, :, :], siluT[:, :, :]))
                nc.vector.tensor_tensor(siluT[:, :, :], siluT[:, :, :], cT[:, :, :].rearrange("p b t -> p t b"),
                                        ALU.mult).then_inc(s_silu, 1)

                def statistics(b):
                    dve.wait_ge(s_x[b], 16)
                    for t in range(b * NT, (b + 1) * NT):
                        last = nc.vector.bn_stats(stats[:, t, :], acc[:, t, :])
                    link(last)

                def layer_norm(b):
                    tiles = range(b * NT, (b + 1) * NT)
                    for t in tiles:
                        last = nc.vector.bn_aggr(mv[:, t, :], stats[:, t, :])
                    link(last)
                    nc.vector.tensor_scalar(var[:, b * NT:(b + 1) * NT], mv[:, b * NT:(b + 1) * NT, 1],
                                            EPS, None, ALU.add).then_inc(s_var, 1)
                    dve.wait_ge(s_rstd, b + 1)
                    for t in tiles:
                        dst = (prob[1] if b == 0 else acc)[:, t, :]
                        nc.vector.tensor_scalar(dst, acc[:, t, :], mv[:, t, 0:1], rstd[:, t:t + 1],
                                                ALU.subtract, ALU.mult).then_inc(s_xn, 1)

                def split_input(b):
                    for m in range(b * KT, (b + 1) * KT):
                        dve.wait_ge(s_ht, m + 1)
                        cols = slice(b * S, (b + 1) * S)
                        nc.vector.tensor_copy(hThi[:, m % KT, cols], ht[:, m % HT, :]).then_inc(s_hhi, 1)
                        dve.wait_ge(s_hhi, m + 1)
                        nc.vector.tensor_tensor(hTlo[:, m % KT, cols], ht[:, m % HT, :],
                                                hThi[:, m % KT, cols].bitcast(F32), ALU.subtract).then_inc(s_hlo, 1)

                statistics(0)
                layer_norm(0)
                dve.wait_ge(s_modp, 1)
                modp = PS[5]
                nc.vector.tensor_copy(modT[:, 0, :, :].rearrange("p f b -> p (f b)"), modp[:, 0:KT * B])
                nc.vector.tensor_scalar(modT[:, 1, :, :].rearrange("p f b -> p (f b)"), modp[:, KT * B:2 * KT * B],
                                        1.0, None, ALU.add).then_inc(s_mod, 1)
                for k in range(ITEMS):
                    dve.wait_ge(s_whi, k + 1)
                    nc.vector.tensor_tensor(wqkv["lo"][:, k, :, :], raw_item(k), wqkv["hi"][:, k, :, :].bitcast(F32),
                                            ALU.subtract).then_inc(s_wlo, 1)
                split_input(0)
                dve.wait_ge(s_bias, 48)
                dve.wait_ge(s_const, 16)
                rope(0, 0, K_, A_)
                statistics(1)
                rope(0, 0, QS[0], B_)
                layer_norm(1)
                rope(0, 0, QS[1], B_)
                split_input(1)
                rope(0, 0, QS[2], A_)
                rope(0, 0, QS[3], B_)
                v_low(0, 0)
                rope(0, 1, K_, A_)
                for h in range(R):
                    maximum(0, 0, 0, h)
                    if h % 2:
                        invert(0, 0, 0, h // 2)
                rope(0, 1, QS[0], B_)
                dve.wait_ge(s_bo, 16 * B * NT)
                dve.sem_inc(s_acc, 1)

                def slots(g, b, i, last):
                    items, obank = ahead(g, b, i, last)
                    nxt = following(g, b, i)
                    more = not (last and (b, i) == (B - 1, NT - 1))

                    def top(h):
                        if more:
                            maximum(*nxt, h)
                            if h == 3:
                                invert(*nxt, 1)

                    def ctx_low():
                        dve.wait_ge(s_ctxhi, slot(g, b, i) + 1)
                        nc.vector.tensor_tensor(ctxlo[:, :], ctx_bank[:, :], ctxhi[:, :].bitcast(F32),
                                                ALU.subtract).then_inc(s_ctxlo, 1)

                    def wo_low(k):
                        h = WO_ORDER[k]
                        if (b, i) == (0, 0):
                            dve.wait_ge(s_wohi, g * R + (k + 1))
                            nc.vector.tensor_tensor(wo["lo"][:, h, :], rawo[:, h, :], wo["hi"][:, h, :].bitcast(F32),
                                                    ALU.subtract).then_inc(s_wolo, 1)

                    top(0)
                    top(1)
                    pt_low(g, b, i, 0)
                    top(2)
                    if more:
                        invert(*nxt, 0)
                    wo_low(0)
                    if (b, i) == (0, 0):
                        ctx_low()
                    if i >= 1:
                        pt_low(g, b, i, 1)
                    if i == 3:
                        pt_low(g, b, i, 2)
                    top(3)
                    if i >= 2:
                        pt_low(g, b, i, i)
                    if last and b == 1:
                        row_stats(i + 1)
                        if i >= 1:
                            low_low(i - 1)
                            gate_product(i - 1)
                        rows_low(i)
                    if len(items) > 1:
                        rope(*items[0])
                    wo_low(2)
                    if (b, i) != (0, 0):
                        ctx_low()
                    wo_low(3)
                    if items and items[-1][2] != V_:
                        rope(*items[-1])
                    if last and (b, i) == (0, 3):
                        row_stats(0)
                        base_low(0)
                        base_low(1)
                        norm_rows(0)
                    if last and b == 1:
                        norm_rows(i + 1)
                        route(i)
                    dve.wait_ge(s_o, slot(g, b, i) + 1)
                    a = acc[:, b * NT + i, :]
                    nc.vector.tensor_tensor(a, obank[:, :], a, ALU.add).then_inc(s_acc, 1)
                    if items and items[0][2] == V_:
                        v_low(items[0][0], items[0][1])
                    k = bc_before(b, i)
                    if last and more and bc_before(*nxt[1:]) > k:
                        if k == 2:
                            dve.wait_ge(s_qklo, G * B * ROPES)
                        copy_row(k)
                        if k in (0, 2):
                            repeat(k + 1)
                    if last and b == 0 and i in VECTORS:
                        copy_vectors(i)
                        if i == 0:
                            dve.wait_ge(s_vtr, G * B)
                        if i != 1:
                            repeat(i)
                    if last and (b, i) == (1, 0):
                        base_low(2)
                        base_low(3)
                        bias_row(0)
                        bias_row(1)
                    if last and b == 1:
                        weigh(i)

                with dve.Fori(0, G - 1) as g:
                    for b in range(B):
                        for i in range(NT):
                            slots(g, b, i, False)
                for b in range(B):
                    for i in range(NT):
                        slots(G - 1, b, i, True)
                row_stats(NT + 1)
                low_low(NT - 1)
                norm_rows(NT + 1)
                rows_low(NT)
                row_stats(NT + 2)
                gate_product(NT - 1)
                norm_rows(NT + 2)
                for m in range(NT, NM):
                    route(m)
                    if m + 1 < NM:
                        rows_low(m + 1)
                    if m == NT:
                        row_stats(NT + 3)
                        norm_rows(NT + 3)
                    weigh(m)
                    if m > NT:
                        gate_product(m - 1)
                    low_low(m)
                gate_product(NM - 1)
                m = NM - 1
                dve.wait_ge(t_prod, NM)
                dve.wait_ge(t_pool, 2 * NM)
                nc.vector.tensor_tensor(acc[:, m, :], acc[:, m, :], ring[m % RING], ALU.add).then_inc(t_outlast, 1)


def kernel(**inputs):
    import numpy as np
    import concourse.bacc as bacc
    from concourse.bass_utils import run_bass_kernel_spmd

    a = {k.replace("L0_", "", 1): np.asarray(v) for k, v in inputs.items()}
    half = D // 2
    inv_freq = (np.float32(1.0) / np.float32(10000.0) ** (np.arange(half, dtype=np.float32) / np.float32(half))).astype(np.float32)
    ang = (inv_freq[:, None] * np.arange(S, dtype=np.float32)[None, :]).astype(np.float32)
    cos, sin = np.cos(ang).astype(np.float32), np.sin(ang).astype(np.float32)
    consts = np.zeros((P, 3 * S + P), np.float32)
    consts[:, 0:S] = np.concatenate([cos, cos])
    consts[:, S:2 * S] = np.concatenate([sin, -sin])
    consts[:, 3 * S - P:3 * S] = np.where(np.arange(P)[None, :] > np.arange(P)[:, None], np.float32(MASKED), 0)
    consts[:, 3 * S:] = np.eye(P, dtype=np.float32)

    def by_group(w, n):
        return w.reshape(KT, P, G, n).transpose(2, 1, 0, 3)

    arrays = {
        "x": a["attn_hidden_states"],
        "Wq": by_group(a["attn_Wq"], R * D), "Wk": by_group(a["attn_Wk"], D), "Wv": by_group(a["attn_Wv"], D),
        "Wo": a["attn_Wo"].reshape(G, R, D, HID).transpose(0, 2, 1, 3),
        "bq": a["attn_bq"].reshape(H, D).T, "bk": a["attn_bk"].reshape(G, D).T, "bv": a["attn_bv"].reshape(G, D).T,
        "bo": a["attn_bo"].reshape(1, HID),
        "gateT": a["ffn_gate_w"].T, "baseT": a["ffn_base_w"].T, "base_b": a["ffn_base_b"].reshape(1, HID),
        "loraAT": a["ffn_lora_A"].reshape(E * RANK, HID).T, "loraB": a["ffn_lora_B"].transpose(0, 2, 1).reshape(E * RANK, HID),
        "c": a["c"], "wmod": a["wmod"], "consts": consts, "iota8": np.arange(E, dtype=np.float32).reshape(1, E),
    }
    nc = bacc.Bacc("TRN2", target_bir_lowering=False, num_devices=1)
    data, args = {}, []
    for name, v in arrays.items():
        v = np.ascontiguousarray(v)
        data[f"in_{name}"] = v
        args.append(nc.dram_tensor(f"in_{name}", v.shape, mybir.dt.from_np(v.dtype), kind="ExternalInput").ap())
    out = nc.dram_tensor("out", (B, S, HID), F32, kind="ExternalOutput").ap()
    adaln_block(nc, *args, out)
    r = run_bass_kernel_spmd(nc, [data], core_ids=[0])
    return r.results[0]["out"]
```

```python
from contextlib import ExitStack

import concourse.bass as bass
from concourse import mybir

B, S, HID = 2, 512, 512
H, G, D = 32, 8, 128
R = H // G
P = 128
KT = HID // P
NT = S // P
E, RANK = 8, 16
EPS = 1e-5
SCALE = float(D) ** -0.5
MASKED = -(2.0 ** 127)
SLOTS = B * NT
TRI = [0, 1, 3, 6, 10]
ITEMS = 2 + R
ROPES = 1 + R
K_, V_ = 0, 2
QS = [1, 3, 4, 5]
LORA_PAD = 256
NM = B * NT
VECTORS = 6
SPLIT_AT = {(0, 0): [0, 1], (0, 3): [2], (1, 0): [3, 4, 5]}
FILLS = [(2, 0, 2), (2, 0, 2), (2, 1, 2, 3), (3, 0, 1, 1, 3)]
WO_ORDER = [0, 3, 1, 2]
WO_POOL = 1
CTX_HALVES = [slice(0, 2 * P), slice(2 * P, 4 * P)]

F32 = mybir.dt.float32
F32R = mybir.dt.float32r
U32 = mybir.dt.uint32
ALU = mybir.AluOpType
ACT = mybir.ActivationFunctionType


def adaln_block(nc, x, Wq, Wk, Wv, Wo, bq, bk, bv, bo, gateT, baseT, base_b, loraAT, loraB, c, wmod,
                consts, iota8, out):
    ctx = ExitStack()
    with ctx:
        def sb(name, shape, dt=F32, stack=ctx):
            return stack.enter_context(nc.sbuf_tensor(name, shape, dt))

        def sem(name):
            return ctx.enter_context(nc.semaphore(name))

        const = sb("const", [P, 3 * S + P])
        cos = const[:, 0:S]
        sin = const[:, S:2 * S]
        mask = const[:, 2 * S:3 * S]
        ident = const[:, 3 * S:3 * S + P]
        acc = sb("acc", [P, B * NT, HID])
        cT = sb("cT", [P, B, KT])
        siluT = sb("siluT", [P, KT, B])
        modT = sb("modT", [P, VECTORS, KT, B])
        stats = sb("stats", [P, B * NT, 6])
        mv = sb("mv", [P, B * NT, 2])
        var = sb("var", [P, B * NT])
        rstd = sb("rstd", [P, B * NT])
        half = sb("half", [P, B * NT])
        bq_sb = sb("bq_sb", [P, H])
        bk_sb = sb("bk_sb", [P, G])
        bv_sb = sb("bv_sb", [P, G])
        negmax = sb("negmax", [P, 2, R])
        rowsum = sb("rowsum", [P, 2, R])
        rinv = sb("rinv", [P, 2, R])
        gw = sb("gw", [P, KT, E])
        io8 = sb("io8", [P, E])
        top = sb("top", [P, 8])
        topi = sb("topi", [P, 8], U32)
        small = sb("small", [P, 8])
        oneh = sb("oneh", [P, 2, E])
        sign = sb("sign", [P, 2, KT * B])
        size = sb("size", [P, 2, KT * B])
        PS = [ctx.enter_context(nc.psum_tensor(f"bank{k}", [P, 512], F32)) for k in range(8)]
        s_bank = [PS[0], PS[1], PS[2], PS[0]]
        pt_bank = [PS[3], PS[4]]
        ctx_bank = PS[5]
        A_, B_ = PS[6], PS[7]

        s_x = [sem(f"s_x{b}") for b in range(B)]
        s_ident = sem("s_ident")
        s_const, s_c, s_bias, s_bo = sem("s_const"), sem("s_c"), sem("s_bias"), sem("s_bo")
        s_wm = [sem(f"s_wm{v}") for v in range(VECTORS)]
        s_rawk, s_rawv, s_rawq, s_rawo = sem("s_rawk"), sem("s_rawv"), sem("s_rawq"), sem("s_rawo")
        s_expc, s_silu = sem("s_expc"), sem("s_silu")
        s_modp, s_mod = sem("s_modp"), sem("s_mod")
        s_half, s_var, s_rstd = sem("s_half"), sem("s_var"), sem("s_rstd")
        s_dve = sem("s_dve")
        s_xn, s_xnT, s_ht, s_hhi, s_hlo = sem("s_xn"), sem("s_xnT"), sem("s_ht"), sem("s_hhi"), sem("s_hlo")
        s_whi, s_wlo, s_wohi, s_wolo = sem("s_whi"), sem("s_wlo"), sem("s_wohi"), sem("s_wolo")
        s_wolo_pool = sem("s_wolo_pool")
        s_proj, s_rope, s_rot, s_qkhi, s_qklo = sem("s_proj"), sem("s_rope"), sem("s_rot"), sem("s_qkhi"), sem("s_qklo")
        s_vt, s_vtr, s_vhi, s_vlo = sem("s_vt"), sem("s_vtr"), sem("s_vhi"), sem("s_vlo")
        s_scores, s_negmax, s_exp, s_rinv, s_prob = sem("s_scores"), sem("s_negmax"), sem("s_exp"), sem("s_rinv"), sem("s_prob")
        s_pt, s_pthi, s_ptlo = sem("s_pt"), sem("s_pthi"), sem("s_ptlo")
        s_ctx, s_ctxhi, s_ctxlo, s_o, s_acc = sem("s_ctx"), sem("s_ctxhi"), sem("s_ctxlo"), sem("s_o"), sem("s_acc")

        t_x = [sem(f"t_x{m}") for m in range(NM)]
        t_base, t_la, t_lb, t_gw, t_bb = sem("t_base"), sem("t_la"), sem("t_lb"), sem("t_gw"), sem("t_bb")
        t_modcopy, t_mod, t_ncol, t_bc, t_bcd = sem("t_modcopy"), sem("t_mod"), sem("t_ncol"), sem("t_bc"), sem("t_bcd")
        t_lahi, t_lalo, t_lbhi, t_lblo = sem("t_lahi"), sem("t_lalo"), sem("t_lbhi"), sem("t_lblo")
        t_basehi, t_baselo, t_gbb = sem("t_basehi"), sem("t_baselo"), sem("t_gbb")
        t_pool = sem("t_pool")
        t_gated, t_var, t_rstd, t_xn, t_xT = sem("t_gated"), sem("t_var"), sem("t_rstd"), sem("t_xn"), sem("t_xT")
        t_h, t_hhi, t_hlo, t_low = sem("t_h"), sem("t_hhi"), sem("t_hlo"), sem("t_low")
        t_diff, t_e, t_lw, t_lwT, t_lwhi, t_lwlo = (sem("t_diff"), sem("t_e"), sem("t_lw"), sem("t_lwT"),
                                                    sem("t_lwhi"), sem("t_lwlo"))
        t_y, t_prod, t_out, t_outlast, t_done = sem("t_y"), sem("t_prod"), sem("t_out"), sem("t_outlast"), sem("t_done")

        with ExitStack() as attn:
            hThi = sb("hThi", [P, KT, B * S], F32R, attn)
            hTlo = sb("hTlo", [P, KT, B * S], F32R, attn)
            wqkv = {hl: sb(f"wqkv{hl}", [P, ITEMS, KT, P], F32R, attn) for hl in ("hi", "lo")}
            wo = {hl: sb(f"wo{hl}", [P, R, HID], F32R, attn) for hl in ("hi", "lo")}
            rawk = sb("rawk", [P, KT, P], F32, attn)
            rawv = sb("rawv", [P, KT, P], F32, attn)
            rawq = sb("rawq", [P, KT, R * P], F32, attn)
            rawo = sb("rawo", [P, R, HID], F32, attn)
            qkhi = sb("qkhi", [P, 2, ROPES, S], F32R, attn)
            qklo = sb("qklo", [P, 2, ROPES, S], F32R, attn)
            vt = sb("vt", [P, S], F32, attn)
            vhi = sb("vhi", [P, 2, NT, P], F32R, attn)
            vlo = sb("vlo", [P, 2, NT, P], F32R, attn)
            prob = [sb("prob0", [P, R, 3 * P], F32, attn), sb("prob1", [P, R, 4 * P], F32, attn)]
            pthi = sb("pthi", [P, NT, R * P], F32R, attn)
            ptlo = sb("ptlo", [P, NT, R * P], F32R, attn)
            ctxhi = sb("ctxhi", [P, R * P], F32R, attn)
            ctxlo = sb("ctxlo", [P, R * P], F32R, attn)
            ropeA = sb("ropeA", [P, 2, S], F32, attn)
            ropeB = sb("ropeB", [P, 2, S], F32, attn)
            ht = prob[0][:, :, :].rearrange("p a n -> p (a n)").rearrange("p (a n) -> p a n", n=S)
            HT = 3

            halves = [ropeA[:, :, :], ropeB[:, :, :]]
            wmt = {0: [rawo[:, :, :]], 1: halves, 2: [rawo[:, :, :]], 3: halves, 4: [rawo[:, :, :]],
                   5: [prob[1][:, :, :]]}
            def flat(buf):
                return buf.rearrange("p a n -> p (a n)")

            baser = rawq
            base = {"hi": hThi[:, :, 0:HID], "lo": hTlo[:, :, 0:HID]}
            lar = rawo[:, 0, :].rearrange("p (t n) -> p t n", t=KT)
            la = {"hi": hThi[:, :, S:S + LORA_PAD], "lo": hTlo[:, :, S:S + LORA_PAD]}
            lbr = rawo[:, 1, :]
            lb = {hl: flat(wqkv[hl][:, V_, :, :]) for hl in ("hi", "lo")}
            xs = [rawo[:, 2, :], rawo[:, 3, :], rawq[:, 2, :], rawq[:, 3, :],
                  rawo[:, 0, :], rawo[:, 1, :], rawo[:, 2, :], rawo[:, 3, :]]
            bb = rawq[:, 0, :]
            ga_rows = [flat(rawk[:, :, :]), flat(rawv[:, :, :])]
            gb_rows = [ropeA[:, 0, :], ropeA[:, 1, :]]
            gbb = [cos, sin]
            ncol = vt[:, :].rearrange("p (f n) -> p f n", f=KT)
            ring = [ropeB[:, 0, :], ropeB[:, 1, :], vt[:, :], rawq[:, 0, :]]
            RING = len(ring)

            def h2(m):
                return ring[m % RING].rearrange("p (f n) -> p f n", f=KT)

            def h2s(hl, m):
                return wqkv[hl][:, (K_, QS[0], QS[2], QS[3])[m % RING], :, :]

            def lw(m):
                return rawq[:, 1, (m % 2) * P:(m % 2 + 1) * P]

            def lws(hl, m):
                return wqkv[hl][:, QS[1], m % 2, :]

            xT_bank = [ctx_bank] * (NT + 1) + [PS[0], PS[1], PS[2]]
            low_bank = [A_] * NT + [PS[3], PS[4], PS[5], PS[3]]
            lwT_bank = [B_] * NT + low_bank[NT:]
            y_bank = [A_] * NT + [B_, A_] * 2
            bc_bank = PS[1]
            modp = PS[5]

            def raw_item(k):
                if k == K_:
                    return rawk[:, :, :]
                if k == V_:
                    return rawv[:, :, :]
                return rawq[:, :, QS.index(k) * P:(QS.index(k) + 1) * P]

            def wait_raw(eng, g, k):
                eng.wait_ge(s_rawk if k == K_ else s_rawv if k == V_ else s_rawq, 16 * g + 16)

            def slot(g, b, i):
                return g * SLOTS + (NT * b + i)

            def unit(g, b):
                return g * B + b

            def pts(g, b, i):
                return g * (2 * TRI[NT]) + (b * TRI[NT] + TRI[i])

            def following(g, b, i):
                i += 1
                if i == NT:
                    i, b = 0, b + 1
                if b == B:
                    b, g = 0, g + 1
                return g, b, i

            def ahead(g, b, i, last):
                if last and b == 1:
                    return [], B_
                if i == NT - 1:
                    return ([] if last else [(g + 1, b, K_, A_), (g + 1, b, QS[0], B_)]), A_
                gn, bn = (g, 1) if b == 0 else (g + 1, 0)
                return {0: ([(gn, bn, V_, B_)], A_),
                        1: ([(gn, bn, QS[1], B_)], A_),
                        2: ([(gn, bn, QS[2], B_), (gn, bn, QS[3], A_)], B_)}[i]

            def late(g, b, i, last):
                if i == 0 and not (last and b == 1):
                    return ((g, 1) if b == 0 else (g + 1, 0)) + (QS[0],)
                if i == 3 and not (last and b == 1):
                    return ((g, 1) if b == 0 else (g + 1, 0)) + (QS[3],)
                return None

            def last_group(g):
                return isinstance(g, int) and g == G - 1

            def bc_before(b, i):
                return min(max(NT * b + i - 1, 0), 2 * B)

            def rope_no(k):
                return 0 if k == K_ else 1 + QS.index(k)

            def parity(b, r):
                return (b * ROPES + r) % 2

            main = attn.enter_context(nc.Block())

            @main.sync
            def _(sp):
                xv = x.rearrange("b (t p) n -> b p t n", p=P)
                sp.dma_start(cT[:, :, :], c.rearrange("b (p t) -> p b t", t=KT)).then_inc(s_c, 16)
                wms = wmod.rearrange("(p t) n -> p t n", t=KT)

                def wm_load(v):
                    t = 0
                    for part in wmt[v]:
                        n = part.shape[1]
                        sp.dma_start(part, wms[:, t:t + n, v * HID:(v + 1) * HID]).then_inc(s_wm[v], 16)
                        t += n

                wm_load(0)
                wm_load(1)
                sp.dma_start(acc[:, 0:NT, :], xv[0]).then_inc(s_x[0], 16)
                sp.dma_start(const[:, 3 * S:], consts[:, 3 * S:]).then_inc(s_ident, 16)
                sp.dma_start(bq_sb[:, :], bq).then_inc(s_bias, 16)
                sp.dma_start(bk_sb[:, :], bk).then_inc(s_bias, 16)
                sp.dma_start(bv_sb[:, :], bv).then_inc(s_bias, 16)
                sp.dma_start(rawk[:, :, :], Wk[0]).then_inc(s_rawk, 16)
                sp.dma_start(rawq[:, :, :], Wq[0]).then_inc(s_rawq, 16)
                sp.dma_start(rawv[:, :, :], Wv[0]).then_inc(s_rawv, 16)
                sp.wait_ge(s_modp, 1)
                wm_load(2)
                sp.dma_start(acc[:, NT:2 * NT, :], xv[1]).then_inc(s_x[1], 16)
                sp.wait_ge(s_modp, 2)
                wm_load(3)
                sp.dma_start(const[:, 0:3 * S], consts[:, 0:3 * S]).then_inc(s_const, 16)
                sp.wait_ge(s_xnT, KT)
                wm_load(5)
                sp.wait_ge(s_modp, 3)
                wm_load(4)
                sp.wait_ge(s_modp, 5)
                sp.dma_start(rawo[:, :, :], Wo[0]).then_inc(s_rawo, 16)
                sp.wait_ge(s_xnT, B * KT)
                for t in range(B * NT):
                    sp.dma_start(acc[:, t, :], bo.broadcast_to([P, HID])).then_inc(s_bo, 16)

                def loads(g):
                    sp.wait_ge(s_wlo, g * ITEMS + ITEMS)
                    sp.dma_start(rawk[:, :, :], Wk[bass.ds(g + 1, 1)]).then_inc(s_rawk, 16)
                    sp.dma_start(rawv[:, :, :], Wv[bass.ds(g + 1, 1)]).then_inc(s_rawv, 16)
                    sp.dma_start(rawq[:, :, :], Wq[bass.ds(g + 1, 1)]).then_inc(s_rawq, 16)
                    sp.wait_ge(s_wolo, g * (R - 1) + (R - 1))
                    sp.wait_ge(s_wolo_pool, g + 1)
                    sp.dma_start(rawo[:, :, :], Wo[bass.ds(g + 1, 1)]).then_inc(s_rawo, 16)

                with sp.Fori(0, G - 1) as g:
                    loads(g)
                sp.wait_ge(s_bo, 16 * B * NT)
                xt = x.rearrange("b (t p) n -> (b t) p n", p=P)
                ot = out.rearrange("b (t p) n -> (b t) p n", p=P)

                def x_load(m):
                    sp.dma_start(xs[m], xt[m]).then_inc(t_x[m], 16)

                sp.wait_ge(s_wlo, G * ITEMS)
                sp.dma_start(baser[:, :, :], baseT.rearrange("(t p) n -> p t n", p=P)).then_inc(t_base, 16)
                sp.dma_start(gw[:, :, :], gateT.rearrange("(t p) n -> p t n", p=P)).then_inc(t_gw, 16)
                sp.dma_start(io8[:, :], iota8.broadcast_to([P, E])).then_inc(t_gw, 16)
                sp.wait_ge(s_wolo, G * (R - 1))
                sp.wait_ge(s_wolo_pool, G)
                x_load(0)
                x_load(1)
                sp.dma_start(lar, loraAT.rearrange("(t p) n -> p t n", p=P)).then_inc(t_la, 16)
                sp.dma_start(lbr, loraB).then_inc(t_lb, 16)
                sp.wait_ge(t_baselo, KT)
                x_load(2)
                sp.dma_start(bb, base_b.broadcast_to([P, HID])).then_inc(t_bb, 16)
                x_load(3)
                sp.wait_ge(t_lalo, 1)
                x_load(4)
                sp.wait_ge(t_lblo, 1)
                x_load(5)
                for m in (6, 7):
                    sp.wait_ge(t_xT, m - 5)
                    x_load(m)
                for m in range(NM):
                    if m < NM - 1:
                        sp.wait_ge(t_out, m + 1)
                    else:
                        sp.wait_ge(t_outlast, 1)
                    sp.dma_start(ot[m], acc[:, m, :]).then_inc(t_done, 16)
                sp.wait_ge(t_done, 16 * NM)

            @main.tensor
            def _(pe):
                def three(out, whi, wlo, xhi, xlo, start, stop):
                    nc.tensor.matmul(out, whi, xhi, start=start, stop=False)
                    nc.tensor.matmul(out, whi, xlo, start=False, stop=False)
                    return nc.tensor.matmul(out, wlo, xhi, start=False, stop=stop)

                def project(g, b, k, bank, tiles=range(KT)):
                    if tiles[0] == 0:
                        pe.wait_ge(s_wlo, g * ITEMS + (k + 1))
                    for t in tiles:
                        last = three(bank[:, :], wqkv["hi"][:, k, t, :], wqkv["lo"][:, k, t, :],
                                     hThi[:, t, b * S:(b + 1) * S], hTlo[:, t, b * S:(b + 1) * S],
                                     t == 0, t == KT - 1)
                    if tiles[-1] == KT - 1:
                        last.then_inc(s_proj, 1)

                def turn_v(g, b):
                    pe.wait_ge(s_vt, unit(g, b) + 1)
                    for t in range(NT):
                        last = nc.tensor.transpose(pt_bank[1][:, t * P:(t + 1) * P], vt[:, t * P:(t + 1) * P], ident)
                    last.then_inc(s_vtr, 1)

                def scores(g, b, i, h, first=False):
                    n = slot(g, b, i)
                    if i == 0:
                        pe.wait_ge(s_qklo, unit(g, b) * ROPES + (h + 2))
                    if last_group(g) and h == 1 and bc_before(b, i - 1):
                        pe.wait_ge(t_bcd, bc_before(b, i - 1))
                    if not first or h == 3:
                        pe.wait_ge(s_exp, {0: n * R, 1: n * R - 2, 2: n * R - 1, 3: n * R + 1}[h])
                    w = max(2, i + 1) * P
                    q = slice(i * P, (i + 1) * P)
                    three(s_bank[h][:, 0:w], qkhi[:, b, 1 + h, q], qklo[:, b, 1 + h, q],
                          qkhi[:, b, 0, 0:w], qklo[:, b, 0, 0:w], True, True).then_inc(s_scores, 1)

                def turn(g, b, i, j):
                    if j == 0:
                        pe.wait_ge(s_prob, slot(g, b, i) * R + R)
                    if j == 1 and i == 1 and not (last_group(g) and b == 1):
                        pe.wait_ge(s_vlo, unit(g, b) + 2)
                    if j >= 2:
                        pe.wait_ge(s_ptlo, pts(g, b, i) + (j - 1))
                    for h in range(R):
                        last = nc.tensor.transpose(pt_bank[j % 2][:, h * P:(h + 1) * P],
                                                   prob[i % 2][:, h, j * P:(j + 1) * P], ident)
                    last.then_inc(s_pt, 1)

                def values(g, b, i, tiles):
                    if last_group(g) and b == 1 and tiles[0] == 0:
                        pe.wait_ge(t_h, KT * (i + 1))
                    for j in tiles:
                        pe.wait_ge(s_ptlo, pts(g, b, i) + (j + 1))
                        last = three(ctx_bank[:, :], vhi[:, b, j, :], vlo[:, b, j, :],
                                     pthi[:, j, :], ptlo[:, j, :], j == 0, j == i)
                    if tiles[-1] == i:
                        last.then_inc(s_ctx, 1)

                def output(g, b, i, bank, between=None):
                    for n, h in enumerate(WO_ORDER if (b, i) == (0, 0) else range(R)):
                        pe.wait_ge(s_ctxlo, slot(g, b, i) * 2 + (h // 2 + 1))
                        if (b, i) == (0, 0):
                            if n == WO_POOL:
                                pe.wait_ge(s_wolo_pool, g + 1)
                            else:
                                pe.wait_ge(s_wolo, g * (R - 1) + (n + 1 if n < WO_POOL else n))
                        if n == 1 and between is not None:
                            pe.wait_ge(s_ctxlo, slot(g, b, i) * 2 + 2)
                            turn_rows(between)
                        last = three(bank[:, :], ctxhi[:, h * P:(h + 1) * P], ctxlo[:, h * P:(h + 1) * P],
                                     wo["hi"][:, h, :], wo["lo"][:, h, :], n == 0, n == R - 1)
                    last.then_inc(s_o, 1)

                def bank_free(g, b, i, items, what):
                    n, ropes = slot(g, b, i), (unit(g, b) + 1) * ROPES
                    if what == "out":
                        if i <= 1 or (b == 1 and not items):
                            pe.wait_ge(s_acc, n + 1)
                        elif i == 2:
                            pe.wait_ge(s_rope, ropes + 4)
                        else:
                            pe.wait_ge(s_rope, ropes + (ROPES + 1 if items else ROPES))
                    elif what == V_:
                        pe.wait_ge(s_rope, ropes + 2)
                    elif what == QS[1]:
                        pe.wait_ge(s_vt, unit(g, b) + 2)
                    elif what == QS[2]:
                        pe.wait_ge(s_rope, ropes + 3)
                    elif what == K_:
                        pe.wait_ge(s_rope, ropes + 5)
                    else:
                        pe.wait_ge(s_acc, n + 1)

                def vector(v):
                    pe.wait_ge(s_wm[v], 16 * len(wmt[v]))
                    each = KT // len(wmt[v])
                    for f in range(KT):
                        for t in range(KT):
                            last = nc.tensor.matmul(modp[:, (v * KT + f) * B:(v * KT + f + 1) * B],
                                                    wmt[v][t // each][:, t % each, f * P:(f + 1) * P],
                                                    siluT[:, t, :], start=t == 0, stop=t == KT - 1)
                    last.then_inc(s_modp, 1)

                pe.wait_ge(s_silu, 1)
                vector(0)
                vector(1)
                pe.wait_ge(s_ident, 16)

                def turn_x(b):
                    for f in range(KT):
                        m = b * KT + f
                        if f == 0:
                            pe.wait_ge(s_xn, (b + 1) * NT)
                        if m >= 4:
                            pe.wait_ge(s_ht, m - 3)
                        for t in range(NT):
                            src = (prob[1] if b == 0 else acc)[:, b * NT + t, f * P:(f + 1) * P]
                            last = nc.tensor.transpose(PS[m % 4][:, t * P:(t + 1) * P], src, ident)
                        last.then_inc(s_xnT, 1)

                turn_x(0)
                pe.wait_ge(s_mod, 1)
                vector(2)
                pe.wait_ge(s_hlo, KT)
                project(0, 0, K_, A_)
                vector(3)
                project(0, 0, QS[0], B_)
                turn_x(1)
                pe.wait_ge(s_rope, 1)
                project(0, 0, V_, A_)
                pe.wait_ge(s_rope, 2)
                project(0, 0, QS[1], B_)
                pe.wait_ge(s_vt, 1)
                project(0, 0, QS[2], A_)
                pe.wait_ge(s_rope, 3)
                project(0, 0, QS[3], B_)
                turn_v(0, 0)
                vector(4)
                pe.wait_ge(s_hlo, 2 * KT)
                pe.wait_ge(s_rope, 4)
                project(0, 1, K_, A_)
                pe.wait_ge(s_rope, 5)
                project(0, 1, QS[0], B_)
                for h in range(R - 1):
                    scores(0, 0, 0, h, first=True)
                vector(5)
                scores(0, 0, 0, R - 1, first=True)
                pe.wait_ge(t_modcopy, 1)

                def broadcast(b, i):
                    pe.wait_ge(s_exp, (slot(G - 1, b, i) + 1) * R + 2)
                    pe.wait_ge(t_ncol, bc_before(b, i) + 1)
                    for f in range(KT):
                        last = nc.tensor.matmul(bc_bank[:, f * P:(f + 1) * P], ncol[:, f, :], ident,
                                                start=True, stop=True)
                    last.then_inc(t_bc, 1)

                def turn_rows(m):
                    pe.wait_ge(t_xn, m + 1)
                    for f in range(KT):
                        last = nc.tensor.transpose(xT_bank[m][:, f * P:(f + 1) * P],
                                                   xs[m][:, f * P:(f + 1) * P], ident)
                    last.then_inc(t_xT, 1)

                def low_rank(m):
                    if m == 0:
                        pe.wait_ge(t_gw, 32)
                        pe.wait_ge(s_acc, slot(G - 1, 1, 0) + 1)
                    elif m < NT:
                        pe.wait_ge(t_prod, m)
                    elif m == NT + 3:
                        pe.wait_ge(t_lwlo, NT + 1)
                    pe.wait_ge(t_h, KT * (m + 1))
                    bank = low_bank[m]
                    for t in range(KT):
                        nc.tensor.matmul(bank[:, LORA_PAD:LORA_PAD + E], h2(m)[:, t, :], gw[:, t, :],
                                         start=t == 0, stop=t == KT - 1)
                    if m == 0:
                        pe.wait_ge(t_lalo, 1)
                    pe.wait_ge(t_hlo, m + 1)
                    for t in range(KT):
                        last = three(bank[:, 0:LORA_PAD], h2s("hi", m)[:, t, :], h2s("lo", m)[:, t, :],
                                     la["hi"][:, t, :], la["lo"][:, t, :], t == 0, t == KT - 1)
                    last.then_inc(t_low, 1)

                def turn_low(m):
                    pe.wait_ge(t_lw, m + 1)
                    if m < NT:
                        pe.wait_ge(s_acc, slot(G - 1, 1, m) + 2)
                    nc.tensor.transpose(lwT_bank[m][:, 3 * P:4 * P], lw(m), ident).then_inc(t_lwT, 1)

                def linear(m, tiles=range(KT)):
                    if m == 0:
                        pe.wait_ge(t_baselo, KT)
                    if m > NT:
                        if tiles[0] == 0:
                            pe.wait_ge(t_prod, m - 1)
                    elif m == NT:
                        pe.wait_ge(t_lwlo, NT)
                    for t in tiles:
                        three(y_bank[m][:, :], h2s("hi", m)[:, t, :], h2s("lo", m)[:, t, :],
                              base["hi"][:, t, :], base["lo"][:, t, :], t == 0, False)

                def experts(m):
                    if m == 0:
                        pe.wait_ge(t_lblo, 1)
                    pe.wait_ge(t_lwlo, m + 1)
                    three(y_bank[m][:, :], lws("hi", m), lws("lo", m), lb["hi"], lb["lo"], False, True)\
                        .then_inc(t_y, 1)

                def slots(g, b, i, last):
                    second = last and b == 1
                    items, obank = ahead(g, b, i, last)
                    nxt = following(g, b, i)
                    more = not (last and (b, i) == (B - 1, NT - 1))
                    parts = [(item, t) for item in items for t in range(KT)]

                    def fill(n):
                        for item, t in parts[:n]:
                            if t == 0:
                                bank_free(g, b, i, items, item[2])
                            project(*item, range(t, t + 1))
                        del parts[:n]

                    def fill_rows(step, m):
                        if second and m >= 0:
                            step(m)

                    def score(h):
                        if more:
                            scores(*nxt, h)

                    score(0)
                    turn(g, b, i, 0)
                    score(1)
                    if i >= 1:
                        turn(g, b, i, 1)
                    fill_rows(turn_low, i - 1)
                    score(2)
                    fill(FILLS[i][0])
                    if i == 3:
                        turn(g, b, i, 2)
                    score(3)
                    if i == 2:
                        turn(g, b, i, 2)
                    fill(FILLS[i][1])
                    if i == 3:
                        turn(g, b, i, 3)
                        fill(FILLS[i][2])
                    fill_rows(linear, i - 1)
                    values(g, b, i, range(0, min(i + 1, 2)))
                    fill_rows(experts, i - 1)
                    if i >= 2:
                        fill(FILLS[i][-2])
                        values(g, b, i, range(2, i + 1))
                    fill(FILLS[i][-1])
                    fill_rows(low_rank, i)
                    bank_free(g, b, i, items, "out")
                    if second:
                        rows = i + 1
                        if i >= 1:
                            pe.wait_ge(t_lwlo, i)
                    else:
                        rows = 0 if last and i == NT - 1 else None
                    output(g, b, i, obank, rows)
                    if items and items[0][2] == V_:
                        turn_v(items[0][0], items[0][1])
                    if last and bc_before(*following(g, b, i)[1:]) > bc_before(b, i) and more:
                        broadcast(b, i)

                with pe.Fori(0, G - 1) as g:
                    for b in range(B):
                        for i in range(NT):
                            slots(g, b, i, False)
                for b in range(B):
                    for i in range(NT):
                        slots(G - 1, b, i, True)
                low_rank(NT)
                turn_low(NT - 1)
                turn_rows(NT + 1)
                linear(NT - 1)
                experts(NT - 1)
                for m in range(NT, NM):
                    if m + 1 < NM:
                        low_rank(m + 1)
                        if m + 2 < NM:
                            turn_rows(m + 2)
                        linear(m, range(0, 2))
                        turn_low(m)
                        linear(m, range(2, KT))
                    else:
                        linear(m)
                        turn_low(m)
                    experts(m)

            @main.scalar
            def _(act):
                def whi(g, k):
                    wait_raw(act, g, k)
                    nc.scalar.activation(wqkv["hi"][:, k, :, :], raw_item(k), ACT.Copy).then_inc(s_whi, 1)

                def qk_high(g, b, k):
                    r = rope_no(k)
                    act.wait_ge(s_rot, unit(g, b) * ROPES + (r + 1))
                    nc.scalar.activation(qkhi[:, b, r, :], ropeA[:, parity(b, r), :], ACT.Copy).then_inc(s_qkhi, 1)

                def v_copy(g, b):
                    act.wait_ge(s_proj, unit(g, b) * ITEMS + (V_ + 1))
                    nc.scalar.activation(vt[:, :], A_[:, :] if prologue else B_[:, :], ACT.Identity,
                                         bias=bv_sb[:, bass.ds(g, 1)]).then_inc(s_vt, 1)

                def v_high(g, b):
                    act.wait_ge(s_vtr, unit(g, b) + 1)
                    nc.scalar.activation(vhi[:, b, :, :], pt_bank[1][:, :].rearrange("p (t d) -> p t d", t=NT),
                                         ACT.Copy).then_inc(s_vhi, 1)

                def exponent(g, b, i, h):
                    act.wait_ge(s_negmax, slot(g, b, i) * R + (h + 1))
                    nc.scalar.activation(prob[i % 2][:, h, 0:(i + 1) * P], s_bank[h][:, 0:(i + 1) * P], ACT.Exp,
                                         bias=negmax[:, i % 2, h:h + 1], scale=-1.0,
                                         accum_out=rowsum[:, i % 2, h:h + 1]).then_inc(s_exp, 1)

                def pt_high(g, b, i, j):
                    act.wait_ge(s_pt, pts(g, b, i) + (j + 1))
                    nc.scalar.activation(pthi[:, j, :], pt_bank[j % 2][:, :], ACT.Copy).then_inc(s_pthi, 1)

                def base_high(t):
                    act.wait_ge(t_base, 16)
                    nc.scalar.activation(base["hi"][:, t, :], baser[:, t, :], ACT.Copy).then_inc(t_basehi, 1)

                def repeat(k):
                    nc.scalar.activation(ncol, modT[:, (2, 5)[k // B], :, k % B:k % B + 1].to_broadcast([P, KT, P]),
                                         ACT.Copy).then_inc(t_ncol, 1)

                def copy_row(k):
                    act.wait_ge(t_bc, k + 1)
                    if k == 2:
                        act.wait_ge(s_qklo, G * B * ROPES)
                    nc.scalar.activation((ga_rows + gb_rows)[k], bc_bank[:, :], ACT.Copy).then_inc(t_bcd, 1)

                def modulate_rows(m):
                    act.wait_ge(t_xT, m + 1)
                    if m == 0:
                        act.wait_ge(s_qklo, G * B * ROPES)
                        act.wait_ge(t_mod, 1)
                    elif m == 2:
                        act.wait_ge(t_bc, 2 * B)
                    elif m == 3:
                        act.wait_ge(t_gbb, B)
                    elif m >= RING:
                        act.wait_ge(t_out, m - RING + 1)
                    b = m // NT
                    for f in range(KT):
                        nc.scalar.activation(h2(m)[:, f, :], xT_bank[m][:, f * P:(f + 1) * P], ACT.Identity,
                                             bias=modT[:, 3, f, b:b + 1], scale=modT[:, 4, f, b:b + 1])\
                            .then_inc(t_h, 1)
                    act.wait_ge(t_h, KT * (m + 1))
                    if m >= RING:
                        act.wait_ge(t_y, m - RING + 1)
                    nc.scalar.activation(h2s("hi", m), h2(m), ACT.Copy).then_inc(t_hhi, 1)

                def gate_exp(m):
                    act.wait_ge(t_diff, m + 1)
                    nc.scalar.activation(small[:, 1:2], small[:, 0:1], ACT.Exp).then_inc(t_e, 1)

                def low_high(m):
                    act.wait_ge(t_lwT, m + 1)
                    nc.scalar.activation(lws("hi", m), lwT_bank[m][:, 3 * P:4 * P], ACT.Copy).then_inc(t_lwhi, 1)

                act.wait_ge(s_c, 16)
                nc.scalar.activation(siluT[:, :, :], cT[:, :, :].rearrange("p b t -> p t b"), ACT.Exp, scale=-1.0)\
                    .then_inc(s_expc, 1)
                for k in range(ITEMS):
                    whi(0, k)
                act.wait_ge(s_bias, 48)
                prologue = True

                def modulate(b):
                    act.wait_ge(s_mod, 1)
                    for m in range(b * KT, (b + 1) * KT):
                        if m >= HT:
                            act.wait_ge(s_hlo, m - HT + 1)
                        act.wait_ge(s_xnT, m + 1)
                        nc.scalar.activation(ht[:, m % HT, :], PS[m % 4][:, :], ACT.Identity,
                                             bias=modT[:, 0, m % KT, b:b + 1], scale=modT[:, 1, m % KT, b:b + 1])\
                            .then_inc(s_ht, 1)

                modulate(0)
                qk_high(0, 0, K_)
                modulate(1)
                qk_high(0, 0, QS[0])
                v_copy(0, 0)
                for k in QS[1:]:
                    qk_high(0, 0, k)
                v_high(0, 0)
                qk_high(0, 1, K_)
                prologue = False
                for h in range(R):
                    exponent(0, 0, 0, h)

                def slots(g, b, i, last):
                    items, _ = ahead(g, b, i, last)
                    nxt = following(g, b, i)
                    more = not (last and (b, i) == (B - 1, NT - 1))
                    left = late(g, b, i, last)
                    second = last and b == 1

                    def exp(h):
                        if more:
                            exponent(*nxt, h)

                    def ctx_high():
                        act.wait_ge(s_ctx, slot(g, b, i) + 1)
                        nc.scalar.activation(ctxhi[:, :], ctx_bank[:, :], ACT.Copy).then_inc(s_ctxhi, 1)

                    def next_weights():
                        for k in ([] if last else SPLIT_AT.get((b, i), [])):
                            act.wait_ge(s_proj, g * (2 * ITEMS) + (ITEMS + k + 1))
                            whi(g + 1, k)

                    def wo_high(h):
                        if (b, i) == (0, 0):
                            if h == WO_ORDER[0]:
                                act.wait_ge(s_rawo, 16 * g + 16)
                                act.wait_ge(s_acc, g * SLOTS + 1)
                            nc.scalar.activation(wo["hi"][:, h, :], rawo[:, h, :], ACT.Copy).then_inc(s_wohi, 1)

                    if left:
                        qk_high(*left)
                    exp(0)
                    pt_high(g, b, i, 0)
                    exp(1)
                    wo_high(WO_ORDER[0])
                    wo_high(WO_ORDER[1])
                    if i >= 1:
                        pt_high(g, b, i, 1)
                    if second and i >= 1:
                        low_high(i - 1)
                    exp(2)
                    if (b, i) == (0, 0):
                        ctx_high()
                        wo_high(WO_ORDER[2])
                    if i == 3:
                        pt_high(g, b, i, 2)
                    exp(3)
                    if i >= 2:
                        pt_high(g, b, i, i)
                    wo_high(WO_ORDER[3])
                    if i == 3:
                        next_weights()
                    if last and more and 0 < bc_before(b, i) < bc_before(*nxt[1:]):
                        repeat(bc_before(b, i))
                    if (b, i) != (0, 0):
                        ctx_high()
                    if second:
                        gate_exp(i)
                    if last and (b, i) in ((0, 1), (0, 2)):
                        act.wait_ge(s_proj, (G * B - 1) * ITEMS)
                        base_high(2 * i - 2)
                        base_high(2 * i - 1)
                    if last and (b, i) == (0, 3):
                        act.wait_ge(s_proj, G * B * ITEMS)
                        act.wait_ge(t_la, 16)
                        nc.scalar.activation(la["hi"][:, :, 0:P], lar, ACT.Copy).then_inc(t_lahi, 1)
                        act.wait_ge(t_lb, 16)
                        nc.scalar.activation(lb["hi"], lbr, ACT.Copy).then_inc(t_lbhi, 1)
                        modulate_rows(0)
                    if second:
                        modulate_rows(i + 1)
                    if items and items[0][2] == V_:
                        v_copy(items[0][0], items[0][1])
                        next_weights()
                        v_high(items[0][0], items[0][1])
                        if last:
                            act.wait_ge(t_mod, 1)
                            act.wait_ge(s_vtr, G * B)
                            repeat(0)
                    elif items:
                        qk_high(*items[0][:3])
                    k = bc_before(b, i)
                    if last and more and bc_before(*nxt[1:]) > k:
                        copy_row(k)

                with act.Fori(0, G - 1) as g:
                    for b in range(B):
                        for i in range(NT):
                            slots(g, b, i, False)
                for b in range(B):
                    for i in range(NT):
                        slots(G - 1, b, i, True)
                low_high(NT - 1)
                modulate_rows(NT + 1)
                gate_exp(NT)
                for m in range(NT, NM):
                    if m + 2 < NM:
                        modulate_rows(m + 2)
                    if m + 1 < NM:
                        gate_exp(m + 1)
                    low_high(m)

            @main.gpsimd
            def _(pool):
                def wlow(g, k):
                    pool.wait_ge(s_whi, g * ITEMS + (k + 1))
                    nc.gpsimd.tensor_tensor(wqkv["lo"][:, k, :, :], raw_item(k),
                                            wqkv["hi"][:, k, :, :].bitcast(F32), ALU.subtract).then_inc(s_wlo, 1)

                def rotate(g, b, k):
                    r = rope_no(k)
                    q = parity(b, r)
                    pool.wait_ge(s_rope, unit(g, b) * ROPES + (r + 1))
                    nc.gpsimd.tensor_tensor(ropeA[:, q, :], ropeA[:, q, :], ropeB[:, q, :], ALU.add).then_inc(s_rot, 1)

                def qk_low(g, b, k):
                    r = rope_no(k)
                    pool.wait_ge(s_qkhi, unit(g, b) * ROPES + (r + 1))
                    nc.gpsimd.tensor_tensor(qklo[:, b, r, :], ropeA[:, parity(b, r), :],
                                            qkhi[:, b, r, :].bitcast(F32), ALU.subtract).then_inc(s_qklo, 1)

                def normalise(g, b, i, h):
                    if h % 2 == 0:
                        pool.wait_ge(s_rinv, slot(g, b, i) * 2 + (h // 2 + 1))
                    p = prob[i % 2][:, h, 0:(i + 1) * P]
                    nc.gpsimd.tensor_tensor(p, p, rinv[:, i % 2, h:h + 1].to_broadcast([P, (i + 1) * P]),
                                            ALU.mult).then_inc(s_prob, 1)

                def deviation(b):
                    pool.wait_ge(s_var, b + 1)
                    cols = slice(b * NT, (b + 1) * NT)
                    nc.gpsimd.tensor_tensor(rstd[:, cols], var[:, cols], half[:, cols], ALU.pow).then_inc(s_rstd, 1)

                chain = [0]

                def link(ins):
                    chain[0] += 1
                    ins.then_inc(t_pool, 1)
                    pool.wait_ge(t_pool, chain[0])

                def gated(m):
                    a = acc[:, m, :]
                    pool.wait_ge(s_acc, slot(G - 1, m // NT, m % NT) + 2)
                    pool.wait_ge(t_bcd, m // NT + 1)
                    link(nc.gpsimd.tensor_tensor(a, a, ga_rows[m // NT], ALU.mult))
                    pool.wait_ge(t_x[m], 16)
                    nc.gpsimd.tensor_tensor(a, a, xs[m], ALU.add).then_inc(t_gated, 1)

                def deviation_rows(m):
                    pool.wait_ge(t_var, m + 1)
                    nc.gpsimd.tensor_tensor(rstd[:, m:m + 1], var[:, m:m + 1], half[:, m:m + 1], ALU.pow)\
                        .then_inc(t_rstd, 1)

                def add_bias(m):
                    pool.wait_ge(t_gbb, m // NT + 1)
                    pool.wait_ge(t_xn, m + 1)
                    link(nc.gpsimd.tensor_tensor(acc[:, m, :], acc[:, m, :], gbb[m // NT], ALU.add))

                def finish(m):
                    pool.wait_ge(t_prod, m + 1)
                    nc.gpsimd.tensor_tensor(acc[:, m, :], acc[:, m, :], ring[m % RING], ALU.add).then_inc(t_out, 1)

                nc.gpsimd.memset(half[:, :], -0.5).then_inc(s_half, 1)
                pool.wait_ge(s_half, 1)
                deviation(0)
                for k in range(ITEMS):
                    wlow(0, k)
                deviation(1)
                for k in [K_] + QS:
                    rotate(0, 0, k)
                    qk_low(0, 0, k)
                rotate(0, 1, K_)
                qk_low(0, 1, K_)
                rotate(0, 1, QS[0])
                for h in range(R):
                    normalise(0, 0, 0, h)

                def slots(g, b, i, last):
                    items, _ = ahead(g, b, i, last)
                    nxt = following(g, b, i)
                    more = not (last and (b, i) == (B - 1, NT - 1))
                    left = late(g, b, i, last)
                    if left:
                        qk_low(*left)
                    for h in range(R):
                        if more:
                            normalise(*nxt, h)
                        if h == 1 and last and (b, i) == (0, 3):
                            gated(0)
                        if h == 1 and (b, i) == (0, 0):
                            w = WO_ORDER[WO_POOL]
                            pool.wait_ge(s_wohi, g * R + (WO_POOL + 1))
                            nc.gpsimd.tensor_tensor(wo["lo"][:, w, :], rawo[:, w, :], wo["hi"][:, w, :].bitcast(F32),
                                                    ALU.subtract).then_inc(s_wolo_pool, 1)
                    for k in ([] if last else SPLIT_AT.get((b, i), [])):
                        wlow(g + 1, k)
                    if items and items[0][2] != V_:
                        rotate(*items[0][:3])
                        qk_low(*items[0][:3])
                    if len(items) > 1:
                        rotate(*items[1][:3])
                    if last and (b, i) == (0, 3):
                        deviation_rows(0)
                        gated(1)
                        pool.wait_ge(t_lahi, 1)
                        nc.gpsimd.tensor_tensor(la["lo"][:, :, 0:P], lar, la["hi"][:, :, 0:P].bitcast(F32),
                                                ALU.subtract).then_inc(t_lalo, 1)
                        pool.wait_ge(t_lbhi, 1)
                        nc.gpsimd.tensor_tensor(lb["lo"], lbr, lb["hi"].bitcast(F32), ALU.subtract)\
                            .then_inc(t_lblo, 1)
                    if last and b == 1:
                        deviation_rows(i + 1)
                        gated(i + 2)
                        if i >= 1:
                            add_bias(i - 1)
                            finish(i - 1)
                        if i == 3:
                            gated(i + 3)

                with pool.Fori(0, G - 1) as g:
                    for b in range(B):
                        for i in range(NT):
                            slots(g, b, i, False)
                for b in range(B):
                    for i in range(NT):
                        slots(G - 1, b, i, True)
                deviation_rows(NT + 1)
                deviation_rows(NT + 2)
                gated(NT + 3)
                add_bias(NT - 1)
                finish(NT - 1)
                deviation_rows(NT + 3)
                for m in range(NT, NM):
                    add_bias(m)
                    if m < NM - 1:
                        finish(m)

            @main.vector
            def _(dve):
                chain = [0]

                def link(ins):
                    chain[0] += 1
                    ins.then_inc(s_dve, 1)
                    dve.wait_ge(s_dve, chain[0])

                def rope(g, b, k, bank):
                    r = rope_no(k)
                    q = parity(b, r)
                    item = unit(g, b) * ROPES + r
                    if not (isinstance(g, int) and g == 0 and b == 0 and r < 2):
                        dve.wait_ge(s_qklo, item - 1)
                    dve.wait_ge(s_proj, unit(g, b) * ITEMS + (k + 1))
                    if k == K_:
                        lo, hi = bk_sb[0:64, bass.ds(g, 1)], bk_sb[64:128, bass.ds(g, 1)]
                        both = bk_sb[:, bass.ds(g, 1)]
                    else:
                        at = bass.ds(g * R + QS.index(k), 1)
                        lo, hi, both = bq_sb[0:64, at], bq_sb[64:128, at], bq_sb[:, at]
                    nc.vector.scalar_tensor_tensor(out=ropeA[:, q, :], in0=bank[:, :], scalar=both, in1=cos,
                                                   op0=ALU.add, op1=ALU.mult)
                    nc.vector.scalar_tensor_tensor(out=ropeB[0:64, q, :], in0=bank[64:128, :], scalar=hi,
                                                   in1=sin[64:128, :], op0=ALU.add, op1=ALU.mult)
                    nc.vector.scalar_tensor_tensor(out=ropeB[64:128, q, :], in0=bank[0:64, :], scalar=lo,
                                                   in1=sin[0:64, :], op0=ALU.add, op1=ALU.mult).then_inc(s_rope, 1)

                def v_low(g, b):
                    dve.wait_ge(s_vhi, unit(g, b) + 1)
                    nc.vector.tensor_tensor(vlo[:, b, :, :], pt_bank[1][:, :].rearrange("p (t d) -> p t d", t=NT),
                                            vhi[:, b, :, :].bitcast(F32), ALU.subtract).then_inc(s_vlo, 1)

                def maximum(g, b, i, h):
                    w = (i + 1) * P
                    dve.wait_ge(s_scores, slot(g, b, i) * R + (h + 1))
                    dve.nop(nofuse=True)
                    nc.vector.tensor_tensor_reduce(out=s_bank[h][:, 0:w], in0=s_bank[h][:, 0:w], in1=mask[:, S - w:S],
                                                   scale=-SCALE, scalar=3.0e38, op0=ALU.add, op1=ALU.min,
                                                   accum_out=negmax[:, i % 2, h:h + 1]).then_inc(s_negmax, 1)

                def invert(g, b, i, pair):
                    dve.wait_ge(s_exp, slot(g, b, i) * R + (2 * pair + 2))
                    nc.vector.reciprocal(rinv[:, i % 2, 2 * pair:2 * pair + 2],
                                         rowsum[:, i % 2, 2 * pair:2 * pair + 2]).then_inc(s_rinv, 1)

                def pt_low(g, b, i, j):
                    dve.wait_ge(s_pthi, pts(g, b, i) + (j + 1))
                    nc.vector.tensor_tensor(ptlo[:, j, :], pt_bank[j % 2][:, :], pthi[:, j, :].bitcast(F32),
                                            ALU.subtract).then_inc(s_ptlo, 1)

                def copy_vectors():
                    dve.wait_ge(s_modp, VECTORS)
                    nc.vector.tensor_copy(modT[:, 2:6, :, :].rearrange("p v f b -> p (v f b)"),
                                          modp[:, 2 * KT * B:6 * KT * B]).then_inc(t_modcopy, 1)
                    dve.wait_ge(t_modcopy, 1)
                    nc.vector.tensor_scalar(modT[:, 4, :, :], modT[:, 4, :, :], 1.0, None, ALU.add)
                    m = modT[:, 2:6:3, :, :].rearrange("p v f b -> p v (f b)")
                    link(nc.vector.tensor_scalar(sign[:, :, :], m, 0.0, 2.0, ALU.is_ge, ALU.mult))
                    link(nc.vector.tensor_scalar(sign[:, :, :], sign[:, :, :], -1.0, None, ALU.add))
                    link(nc.vector.tensor_tensor(size[:, :, :], sign[:, :, :], m, ALU.mult))
                    link(nc.vector.tensor_scalar(size[:, :, :], size[:, :, :], 0.25, None, ALU.max))
                    nc.vector.tensor_tensor(m, sign[:, :, :], size[:, :, :], ALU.mult).then_inc(t_mod, 1)

                def bias_row(b):
                    dve.wait_ge(t_bb, 16)
                    dve.wait_ge(t_bcd, B + b + 1)
                    nc.vector.tensor_tensor(gbb[b], bb, gb_rows[b], ALU.mult).then_inc(t_gbb, 1)

                def base_low(t):
                    dve.wait_ge(t_basehi, t + 1)
                    nc.vector.tensor_tensor(base["lo"][:, t, :], baser[:, t, :], base["hi"][:, t, :].bitcast(F32),
                                            ALU.subtract).then_inc(t_baselo, 1)

                def row_stats(m):
                    dve.wait_ge(t_gated, m + 1)
                    link(nc.vector.bn_stats(stats[:, m, :], acc[:, m, :]))
                    link(nc.vector.bn_aggr(mv[:, m, :], stats[:, m, :]))
                    nc.vector.tensor_scalar(var[:, m:m + 1], mv[:, m, 1:2], EPS, None, ALU.add).then_inc(t_var, 1)

                def norm_rows(m):
                    dve.wait_ge(t_rstd, m + 1)
                    nc.vector.tensor_scalar(xs[m], acc[:, m, :], mv[:, m, 0:1], rstd[:, m:m + 1],
                                            ALU.subtract, ALU.mult).then_inc(t_xn, 1)

                def rows_low(m):
                    dve.wait_ge(t_hhi, m + 1)
                    nc.vector.tensor_tensor(h2s("lo", m), h2(m), h2s("hi", m).bitcast(F32),
                                            ALU.subtract).then_inc(t_hlo, 1)

                def route(m):
                    dve.wait_ge(t_low, m + 1)
                    if m == 0:
                        dve.wait_ge(t_gw, 32)
                    logits = low_bank[m][:, LORA_PAD:LORA_PAD + E]
                    link(nc.vector.max(top[:, :], logits))
                    link(nc.vector.max_index(topi[:, :], top[:, :], logits))
                    link(nc.vector.tensor_copy(small[:, 4:6], topi[:, 0:2]))
                    nc.vector.tensor_tensor(small[:, 0:1], top[:, 1:2], top[:, 0:1], ALU.subtract).then_inc(t_diff, 1)

                def weigh(m):
                    dve.wait_ge(t_e, m + 1)
                    link(nc.vector.tensor_scalar(small[:, 2:3], small[:, 1:2], 1.0, 0.5, ALU.add, ALU.mult))
                    link(nc.vector.reciprocal(small[:, 2:3], small[:, 2:3]))
                    link(nc.vector.tensor_tensor(small[:, 3:4], small[:, 1:2], small[:, 2:3], ALU.mult))
                    for k in range(2):
                        last = nc.vector.tensor_scalar(oneh[:, k, :], io8[:, :], small[:, 4 + k:5 + k],
                                                       small[:, 2 + k:3 + k], ALU.is_equal, ALU.mult)
                    link(last)
                    link(nc.vector.tensor_tensor(oneh[:, 0, :], oneh[:, 0, :], oneh[:, 1, :], ALU.add))
                    if m >= 2:
                        dve.wait_ge(t_lwT, m - 1)
                    nc.vector.tensor_tensor(lw(m).rearrange("p (e r) -> p e r", e=E),
                                            low_bank[m][:, 0:P].rearrange("p (e r) -> p e r", e=E),
                                            oneh[:, 0, :].unsqueeze(2).to_broadcast([P, E, RANK]), ALU.mult)\
                        .then_inc(t_lw, 1)

                def low_low(m):
                    dve.wait_ge(t_lwhi, m + 1)
                    nc.vector.tensor_tensor(lws("lo", m), lwT_bank[m][:, 3 * P:4 * P], lws("hi", m).bitcast(F32),
                                            ALU.subtract).then_inc(t_lwlo, 1)

                def gate_product(m):
                    if m == 0:
                        dve.wait_ge(t_bcd, 2 * B)
                    dve.wait_ge(t_y, m + 1)
                    nc.vector.tensor_tensor(ring[m % RING], y_bank[m][:, :], gb_rows[m // NT], ALU.mult)\
                        .then_inc(t_prod, 1)

                dve.wait_ge(s_expc, 1)
                link(nc.vector.tensor_scalar(siluT[:, :, :], siluT[:, :, :], 1.0, None, ALU.add))
                link(nc.vector.reciprocal(siluT[:, :, :], siluT[:, :, :]))
                nc.vector.tensor_tensor(siluT[:, :, :], siluT[:, :, :], cT[:, :, :].rearrange("p b t -> p t b"),
                                        ALU.mult).then_inc(s_silu, 1)

                def statistics(b):
                    dve.wait_ge(s_x[b], 16)
                    for t in range(b * NT, (b + 1) * NT):
                        last = nc.vector.bn_stats(stats[:, t, :], acc[:, t, :])
                    link(last)

                def layer_norm(b):
                    tiles = range(b * NT, (b + 1) * NT)
                    for t in tiles:
                        last = nc.vector.bn_aggr(mv[:, t, :], stats[:, t, :])
                    link(last)
                    nc.vector.tensor_scalar(var[:, b * NT:(b + 1) * NT], mv[:, b * NT:(b + 1) * NT, 1],
                                            EPS, None, ALU.add).then_inc(s_var, 1)
                    dve.wait_ge(s_rstd, b + 1)
                    for t in tiles:
                        dst = (prob[1] if b == 0 else acc)[:, t, :]
                        nc.vector.tensor_scalar(dst, acc[:, t, :], mv[:, t, 0:1], rstd[:, t:t + 1],
                                                ALU.subtract, ALU.mult).then_inc(s_xn, 1)

                def split_input(b):
                    for m in range(b * KT, (b + 1) * KT):
                        dve.wait_ge(s_ht, m + 1)
                        cols = slice(b * S, (b + 1) * S)
                        nc.vector.tensor_copy(hThi[:, m % KT, cols], ht[:, m % HT, :]).then_inc(s_hhi, 1)
                        dve.wait_ge(s_hhi, m + 1)
                        nc.vector.tensor_tensor(hTlo[:, m % KT, cols], ht[:, m % HT, :],
                                                hThi[:, m % KT, cols].bitcast(F32), ALU.subtract).then_inc(s_hlo, 1)

                statistics(0)
                layer_norm(0)
                dve.wait_ge(s_modp, 2)
                nc.vector.tensor_copy(modT[:, 0, :, :].rearrange("p f b -> p (f b)"), modp[:, 0:KT * B])
                nc.vector.tensor_scalar(modT[:, 1, :, :].rearrange("p f b -> p (f b)"), modp[:, KT * B:2 * KT * B],
                                        1.0, None, ALU.add).then_inc(s_mod, 1)
                split_input(0)
                statistics(1)
                layer_norm(1)
                dve.wait_ge(s_bias, 48)
                dve.wait_ge(s_const, 16)
                dve.wait_ge(s_modp, 4)
                rope(0, 0, K_, A_)
                rope(0, 0, QS[0], B_)
                split_input(1)
                rope(0, 0, QS[1], B_)
                rope(0, 0, QS[2], A_)
                rope(0, 0, QS[3], B_)
                v_low(0, 0)
                rope(0, 1, K_, A_)
                rope(0, 1, QS[0], B_)
                for h in range(R):
                    maximum(0, 0, 0, h)
                    if h % 2:
                        invert(0, 0, 0, h // 2)
                copy_vectors()
                dve.wait_ge(s_bo, 16 * B * NT)
                dve.sem_inc(s_acc, 1)

                def slots(g, b, i, last):
                    items, obank = ahead(g, b, i, last)
                    nxt = following(g, b, i)
                    more = not (last and (b, i) == (B - 1, NT - 1))

                    def top(h):
                        if more:
                            maximum(*nxt, h)
                            if h == 3:
                                invert(*nxt, 1)

                    def ctx_low():
                        dve.wait_ge(s_ctxhi, slot(g, b, i) + 1)
                        for c in CTX_HALVES:
                            nc.vector.tensor_tensor(ctxlo[:, c], ctx_bank[:, c], ctxhi[:, c].bitcast(F32),
                                                    ALU.subtract).then_inc(s_ctxlo, 1)

                    def wo_low(k):
                        h = WO_ORDER[k]
                        if (b, i) == (0, 0):
                            dve.wait_ge(s_wohi, g * R + (k + 1))
                            nc.vector.tensor_tensor(wo["lo"][:, h, :], rawo[:, h, :], wo["hi"][:, h, :].bitcast(F32),
                                                    ALU.subtract).then_inc(s_wolo, 1)

                    top(0)
                    top(1)
                    pt_low(g, b, i, 0)
                    top(2)
                    if more:
                        invert(*nxt, 0)
                    wo_low(0)
                    if (b, i) == (0, 0):
                        ctx_low()
                    if i >= 1:
                        pt_low(g, b, i, 1)
                        if last and b == 1:
                            low_low(i - 1)
                    if i == 3:
                        pt_low(g, b, i, 2)
                    top(3)
                    if i >= 2:
                        pt_low(g, b, i, i)
                    if last and b == 1:
                        row_stats(i + 1)
                        if i == 1:
                            bias_row(0)
                            bias_row(1)
                        if i >= 1:
                            gate_product(i - 1)
                    if len(items) > 1:
                        rope(*items[0])
                    wo_low(2)
                    if last and (b, i) == (0, 3):
                        row_stats(0)
                    if (b, i) != (0, 0):
                        ctx_low()
                    wo_low(3)
                    if items and items[-1][2] != V_:
                        rope(*items[-1])
                    if last and b == 1:
                        norm_rows(i + 1)
                        route(i)
                        weigh(i)
                    if last and (b, i) == (0, 3):
                        norm_rows(0)
                        for t in range(KT):
                            base_low(t)
                        rows_low(0)
                    if last and b == 1:
                        rows_low(i + 1)
                    dve.wait_ge(s_o, slot(g, b, i) + 1)
                    a = acc[:, b * NT + i, :]
                    nc.vector.tensor_tensor(a, obank[:, :], a, ALU.add).then_inc(s_acc, 1)
                    if items and items[0][2] == V_:
                        v_low(items[0][0], items[0][1])

                with dve.Fori(0, G - 1) as g:
                    for b in range(B):
                        for i in range(NT):
                            slots(g, b, i, False)
                for b in range(B):
                    for i in range(NT):
                        slots(G - 1, b, i, True)
                row_stats(NT + 1)
                low_low(NT - 1)
                norm_rows(NT + 1)
                row_stats(NT + 2)
                route(NT)
                rows_low(NT + 1)
                weigh(NT)
                norm_rows(NT + 2)
                for m in range(NT + 1, NM):
                    if m == NT + 1:
                        row_stats(NT + 3)
                    gate_product(m - 2)
                    route(m)
                    low_low(m - 1)
                    if m == NT + 1:
                        norm_rows(NT + 3)
                    if m + 1 < NM:
                        rows_low(m + 1)
                    weigh(m)
                gate_product(NM - 2)
                low_low(NM - 1)
                gate_product(NM - 1)
                m = NM - 1
                dve.wait_ge(t_prod, NM)
                dve.wait_ge(t_pool, 2 * NM)
                nc.vector.tensor_tensor(acc[:, m, :], acc[:, m, :], ring[m % RING], ALU.add).then_inc(t_outlast, 1)


def kernel(**inputs):
    import numpy as np
    import concourse.bacc as bacc
    from concourse.bass_utils import run_bass_kernel_spmd

    a = {k.replace("L0_", "", 1): np.asarray(v) for k, v in inputs.items()}
    half = D // 2
    inv_freq = (np.float32(1.0) / np.float32(10000.0) ** (np.arange(half, dtype=np.float32) / np.float32(half))).astype(np.float32)
    ang = (inv_freq[:, None] * np.arange(S, dtype=np.float32)[None, :]).astype(np.float32)
    cos, sin = np.cos(ang).astype(np.float32), np.sin(ang).astype(np.float32)
    consts = np.zeros((P, 3 * S + P), np.float32)
    consts[:, 0:S] = np.concatenate([cos, cos])
    consts[:, S:2 * S] = np.concatenate([sin, -sin])
    consts[:, 3 * S - P:3 * S] = np.where(np.arange(P)[None, :] > np.arange(P)[:, None], np.float32(MASKED), 0)
    consts[:, 3 * S:] = np.eye(P, dtype=np.float32)

    def by_group(w, n):
        return w.reshape(KT, P, G, n).transpose(2, 1, 0, 3)

    arrays = {
        "x": a["attn_hidden_states"],
        "Wq": by_group(a["attn_Wq"], R * D), "Wk": by_group(a["attn_Wk"], D), "Wv": by_group(a["attn_Wv"], D),
        "Wo": a["attn_Wo"].reshape(G, R, D, HID).transpose(0, 2, 1, 3),
        "bq": a["attn_bq"].reshape(H, D).T, "bk": a["attn_bk"].reshape(G, D).T, "bv": a["attn_bv"].reshape(G, D).T,
        "bo": a["attn_bo"].reshape(1, HID),
        "gateT": a["ffn_gate_w"].T, "baseT": a["ffn_base_w"].T, "base_b": a["ffn_base_b"].reshape(1, HID),
        "loraAT": a["ffn_lora_A"].reshape(E * RANK, HID).T, "loraB": a["ffn_lora_B"].transpose(0, 2, 1).reshape(E * RANK, HID),
        "c": a["c"], "wmod": a["wmod"], "consts": consts, "iota8": np.arange(E, dtype=np.float32).reshape(1, E),
    }
    nc = bacc.Bacc("TRN2", target_bir_lowering=False, num_devices=1)
    data, args = {}, []
    for name, v in arrays.items():
        v = np.ascontiguousarray(v)
        data[f"in_{name}"] = v
        args.append(nc.dram_tensor(f"in_{name}", v.shape, mybir.dt.from_np(v.dtype), kind="ExternalInput").ap())
    out = nc.dram_tensor("out", (B, S, HID), F32, kind="ExternalOutput").ap()
    adaln_block(nc, *args, out)
    r = run_bass_kernel_spmd(nc, [data], core_ids=[0])
    return r.results[0]["out"]
```
